# Optimizing a Trainium2 kernel written in Bass

```python
import numpy as np
import jax
import jax.numpy as jnp

def _softmax(x, axis=-1):
    return jax.nn.softmax(x, axis=axis)

def _gelu(x):
    return jax.nn.gelu(x, approximate=True)

def _silu(x):
    return jax.nn.silu(x)

def _sigmoid(x):
    return jax.nn.sigmoid(x)

def _layernorm(x, axis=-1, eps=1e-05):
    m = jnp.mean(x, axis=axis, keepdims=True)
    v = jnp.var(x, axis=axis, keepdims=True)
    return (x - m) / jnp.sqrt(v + eps)

def _scatter_add(tgt, idx, src, axis=0):
    return tgt.at[idx].add(src)

def _segment_sum(src, seg, n):
    return jax.ops.segment_sum(src, seg, n)
kernel_name = 'mk_hybrid_d1_jaxref_r4_1887c6'

def setup_inputs(seed: int=0):
    np.random.seed(seed)
    _w = jnp.asarray

    def _L0_attn_a_setup():
        import jax, jax.numpy as jnp
        import numpy as np
        B, T, D = (8, 512, 256)
        H, N = (8, 32)

        def _xavier(key, shape, fan_in, fan_out):
            lim = float(np.sqrt(6.0 / (fan_in + fan_out)))
            return jax.random.uniform(key, shape, jnp.float32, -lim, lim)

        def _reference_tuple_inner(x, W_in, W_k, W_v, W_q, W_beta, b_beta, W_out):
            b, t, d = x.shape
            h, n = b_beta.shape
            xp = jax.nn.silu(jnp.einsum('btd,ed->bte', x, W_in))

            def proj(W):
                return jnp.einsum('btd,md->btm', xp, W).reshape(b, t, h, n).transpose(1, 0, 2, 3)
            k_all = proj(W_k)
            v_all = proj(W_v)
            q_all = proj(W_q)
            beta_all = jax.nn.sigmoid(proj(W_beta) + b_beta)
            S0 = jnp.zeros((b, h, n, n), x.dtype)

            def step(S, inp):
                k, v, q, beta = inp
                kn = k / (jnp.linalg.norm(k, axis=-1, keepdims=True) + 1e-06)
                retrieved = jnp.einsum('bhij,bhj->bhi', S, kn)
                delta = v - retrieved
                S = jnp.tanh(beta[..., None] * S + delta[..., None] * kn[..., None, :])
                Sq = jnp.einsum('bhij,bhj->bhi', S, q)
                out = Sq * jax.nn.silu(Sq)
                return (S, out)
            S_final, outs = jax.lax.scan(step, S0, (k_all, v_all, q_all, beta_all))
            cell_out = outs.transpose(1, 0, 2, 3).reshape(b, t, h * n)
            y = jnp.einsum('btm,dm->btd', cell_out, W_out)
            return (y, S_final)
        key = jax.random.key(seed)
        ks = jax.random.split(key, 8)
        x = jax.random.normal(ks[0], (B, T, D), jnp.float32)
        W_in = _xavier(ks[1], (D, D), D, D)
        W_k = _xavier(ks[2], (H * N, D), N, D)
        W_v = _xavier(ks[3], (H * N, D), N, D)
        W_q = _xavier(ks[4], (H * N, D), N, D)
        W_beta = _xavier(ks[5], (H * N, D), N, D)
        b_beta = jnp.full((H, N), 2.0, jnp.float32)
        W_out = _xavier(ks[6], (D, H * N), H * N, D)
        return {'x': x, 'W_in': W_in, 'W_k': W_k, 'W_v': W_v, 'W_q': W_q, 'W_beta': W_beta, 'b_beta': b_beta, 'W_out': W_out}
    _L0_attn_a_in = _L0_attn_a_setup()

    def _L0_attn_b_setup():
        import jax, jax.numpy as jnp
        import numpy as np
        import math
        DIM = 256
        HEADS = 16
        HEAD_DIM = DIM // HEADS
        B, N = (1, 1024)
        key = jax.random.key(seed)
        k1, k2, k3, k4 = jax.random.split(key, 4)
        content = jax.random.normal(k1, (B, N, DIM), dtype=jnp.float32)
        Wq = jnp.eye(DIM, dtype=jnp.float32) + 0.02 * jax.random.normal(k2, (DIM, DIM), dtype=jnp.float32)
        Wk = jnp.eye(DIM, dtype=jnp.float32) + 0.02 * jax.random.normal(k3, (DIM, DIM), dtype=jnp.float32)
        Wv = jnp.eye(DIM, dtype=jnp.float32) + 0.02 * jax.random.normal(k4, (DIM, DIM), dtype=jnp.float32)
        return {'content': content, 'Wq': Wq, 'Wk': Wk, 'Wv': Wv}
    _L0_attn_b_in = _L0_attn_b_setup()

    def _L0_ffn_setup():
        import jax, jax.numpy as jnp
        import numpy as np
        DIM = 256
        NUM_HEAVY = 256
        N_ITERS = 50
        EPS = 1.0
        FETCH_K_RATIO = 9.0 / 8.0

        def rms_norm(x, gamma):
            norm = jnp.maximum(jnp.linalg.norm(x, axis=-1, keepdims=True), 1e-12)
            return x / norm * x.shape[-1] ** 0.5 * gamma

        def feed_forward(x, gamma, w1, b1, w2, b2):
            h = jax.nn.gelu(rms_norm(x, gamma) @ w1 + b1, approximate=False)
            return h @ w2 + b2

        def coor_descent(s, k, n_iters, eps):
            logk = jnp.log(jnp.asarray(k, dtype=s.dtype))

            def step(ab, _):
                a, b = ab
                sb = (s + b) / eps
                a = eps * (logk - jax.scipy.special.logsumexp(sb, axis=-1, keepdims=True))
                b = -jax.nn.relu(s + a)
                return ((a, b), None)
            a0 = jnp.zeros_like(s[..., :1])
            b0 = -s
            (a, b), _ = jax.lax.scan(step, (a0, b0), None, length=n_iters)
            return jnp.exp((s + a + b) / eps)
        key = jax.random.key(seed)
        ks = jax.random.split(key, 8)
        b, n, d = (4, 2048, DIM)
        dl, dh = (int(d * 0.5), d * 4)
        u = lambda k, shape, fan_in: jax.random.uniform(k, shape, jnp.float32, -1.0, 1.0) / np.sqrt(fan_in)
        return {'x': jax.random.normal(ks[0], (b, n, d), jnp.float32), 'routing_token': jax.random.normal(ks[1], (d,), jnp.float32), 'light_gamma': jnp.ones((d,), jnp.float32), 'light_w1': u(ks[2], (d, dl), d), 'light_b1': jnp.zeros((dl,), jnp.float32), 'light_w2': u(ks[3], (dl, d), dl), 'light_b2': jnp.zeros((d,), jnp.float32), 'heavy_gamma': jnp.ones((d,), jnp.float32), 'heavy_w1': u(ks[4], (d, dh), d), 'heavy_b1': jnp.zeros((dh,), jnp.float32), 'heavy_w2': u(ks[5], (dh, d), dh), 'heavy_b2': jnp.zeros((d,), jnp.float32)}
    _L0_ffn_in = _L0_ffn_setup()
    _d = {'L0_attn_a_x': _L0_attn_a_in['x'], 'L0_attn_a_W_in': _L0_attn_a_in['W_in'], 'L0_attn_a_W_k': _L0_attn_a_in['W_k'], 'L0_attn_a_W_v': _L0_attn_a_in['W_v'], 'L0_attn_a_W_q': _L0_attn_a_in['W_q'], 'L0_attn_a_W_beta': _L0_attn_a_in['W_beta'], 'L0_attn_a_b_beta': _L0_attn_a_in['b_beta'], 'L0_attn_a_W_out': _L0_attn_a_in['W_out'], 'L0_attn_b_Wq': _L0_attn_b_in['Wq'], 'L0_attn_b_Wk': _L0_attn_b_in['Wk'], 'L0_attn_b_Wv': _L0_attn_b_in['Wv'], 'L0_ffn_routing_token': _L0_ffn_in['routing_token'], 'L0_ffn_light_gamma': _L0_ffn_in['light_gamma'], 'L0_ffn_light_w1': _L0_ffn_in['light_w1'], 'L0_ffn_light_b1': _L0_ffn_in['light_b1'], 'L0_ffn_light_w2': _L0_ffn_in['light_w2'], 'L0_ffn_light_b2': _L0_ffn_in['light_b2'], 'L0_ffn_heavy_gamma': _L0_ffn_in['heavy_gamma'], 'L0_ffn_heavy_w1': _L0_ffn_in['heavy_w1'], 'L0_ffn_heavy_b1': _L0_ffn_in['heavy_b1'], 'L0_ffn_heavy_w2': _L0_ffn_in['heavy_w2'], 'L0_ffn_heavy_b2': _L0_ffn_in['heavy_b2']}
    _x0 = _d['L0_attn_a_x']
    _d['L0_attn_a_x'] = jax.random.normal(jax.random.fold_in(jax.random.key(seed), 1), (32, 512, 256), dtype=_x0.dtype)
    del _x0
    return _d

def reference(L0_attn_a_x, L0_attn_a_W_in, L0_attn_a_W_k, L0_attn_a_W_v, L0_attn_a_W_q, L0_attn_a_W_beta, L0_attn_a_b_beta, L0_attn_a_W_out, L0_attn_b_Wq, L0_attn_b_Wk, L0_attn_b_Wv, L0_ffn_routing_token, L0_ffn_light_gamma, L0_ffn_light_w1, L0_ffn_light_b1, L0_ffn_light_w2, L0_ffn_light_b2, L0_ffn_heavy_gamma, L0_ffn_heavy_w1, L0_ffn_heavy_b1, L0_ffn_heavy_w2, L0_ffn_heavy_b2):

    def _L0_attn_a_ref(x, W_in, W_k, W_v, W_q, W_beta, b_beta, W_out):
        import jax, jax.numpy as jnp
        import numpy as np
        B, T, D = (8, 512, 256)
        H, N = (8, 32)

        def _xavier(key, shape, fan_in, fan_out):
            lim = float(np.sqrt(6.0 / (fan_in + fan_out)))
            return jax.random.uniform(key, shape, jnp.float32, -lim, lim)

        def _reference_tuple_inner(x, W_in, W_k, W_v, W_q, W_beta, b_beta, W_out):
            b, t, d = x.shape
            h, n = b_beta.shape
            xp = jax.nn.silu(jnp.einsum('btd,ed->bte', x, W_in))

            def proj(W):
                return jnp.einsum('btd,md->btm', xp, W).reshape(b, t, h, n).transpose(1, 0, 2, 3)
            k_all = proj(W_k)
            v_all = proj(W_v)
            q_all = proj(W_q)
            beta_all = jax.nn.sigmoid(proj(W_beta) + b_beta)
            S0 = jnp.zeros((b, h, n, n), x.dtype)

            def step(S, inp):
                k, v, q, beta = inp
                kn = k / (jnp.linalg.norm(k, axis=-1, keepdims=True) + 1e-06)
                retrieved = jnp.einsum('bhij,bhj->bhi', S, kn)
                delta = v - retrieved
                S = jnp.tanh(beta[..., None] * S + delta[..., None] * kn[..., None, :])
                Sq = jnp.einsum('bhij,bhj->bhi', S, q)
                out = Sq * jax.nn.silu(Sq)
                return (S, out)
            S_final, outs = jax.lax.scan(step, S0, (k_all, v_all, q_all, beta_all))
            cell_out = outs.transpose(1, 0, 2, 3).reshape(b, t, h * n)
            y = jnp.einsum('btm,dm->btd', cell_out, W_out)
            return (y, S_final)
        return _reference_tuple_inner(x, W_in, W_k, W_v, W_q, W_beta, b_beta, W_out)[0]

    def _L0_attn_b_ref(content, Wq, Wk, Wv):
        import jax, jax.numpy as jnp
        import numpy as np
        import math
        DIM = 256
        HEADS = 16
        HEAD_DIM = DIM // HEADS
        B, N = (1, 1024)
        b, n, d = content.shape
        Q = (content @ Wq).reshape(b, n, HEADS, HEAD_DIM)
        K = (content @ Wk).reshape(b, n, HEADS, HEAD_DIM)
        V = (content @ Wv).reshape(b, n, HEADS, HEAD_DIM)
        scores = jnp.einsum('bqhd,bkhd->bhqk', Q, K) / math.sqrt(HEAD_DIM)
        alpha = jax.nn.softmax(scores, axis=-1)
        causal = jnp.tril(jnp.ones((n, n), dtype=bool))
        alpha = jnp.where(causal, alpha, jnp.zeros((), dtype=alpha.dtype))
        Y = jnp.einsum('bhqk,bkhd->bqhd', alpha, V).reshape(b, n, d)
        return Y

    def _L0_ffn_ref(x, routing_token, light_gamma, light_w1, light_b1, light_w2, light_b2, heavy_gamma, heavy_w1, heavy_b1, heavy_w2, heavy_b2):
        import jax, jax.numpy as jnp
        import numpy as np
        DIM = 256
        NUM_HEAVY = 256
        N_ITERS = 50
        EPS = 1.0
        FETCH_K_RATIO = 9.0 / 8.0

        def rms_norm(x, gamma):
            norm = jnp.maximum(jnp.linalg.norm(x, axis=-1, keepdims=True), 1e-12)
            return x / norm * x.shape[-1] ** 0.5 * gamma

        def feed_forward(x, gamma, w1, b1, w2, b2):
            h = jax.nn.gelu(rms_norm(x, gamma) @ w1 + b1, approximate=False)
            return h @ w2 + b2

        def coor_descent(s, k, n_iters, eps):
            logk = jnp.log(jnp.asarray(k, dtype=s.dtype))

            def step(ab, _):
                a, b = ab
                sb = (s + b) / eps
                a = eps * (logk - jax.scipy.special.logsumexp(sb, axis=-1, keepdims=True))
                b = -jax.nn.relu(s + a)
                return ((a, b), None)
            a0 = jnp.zeros_like(s[..., :1])
            b0 = -s
            (a, b), _ = jax.lax.scan(step, (a0, b0), None, length=n_iters)
            return jnp.exp((s + a + b) / eps)
        b, n, d = x.shape
        light_out = feed_forward(x, light_gamma, light_w1, light_b1, light_w2, light_b2)
        s = jnp.einsum('bnd,d->bn', x, routing_token)
        effective_k = min(NUM_HEAVY * FETCH_K_RATIO, n)
        scores = coor_descent(s, effective_k, N_ITERS, EPS)
        sel_scores, sel_idx = jax.lax.top_k(scores, NUM_HEAVY)
        sel_scores = sel_scores + jax.lax.stop_gradient(1.0 - sel_scores)
        routed = jnp.take_along_axis(x, sel_idx[..., None], axis=1)
        routed_out = feed_forward(routed, heavy_gamma, heavy_w1, heavy_b1, heavy_w2, heavy_b2)
        routed_out = routed_out * sel_scores[..., None]
        batch_idx = jnp.arange(b)[:, None]
        heavy_out = jnp.zeros_like(x).at[batch_idx, sel_idx].set(routed_out)
        return light_out + heavy_out
    x = L0_attn_a_x
    x = x + _L0_attn_a_ref(_layernorm(x, axis=-1), L0_attn_a_W_in, L0_attn_a_W_k, L0_attn_a_W_v, L0_attn_a_W_q, L0_attn_a_W_beta, L0_attn_a_b_beta, L0_attn_a_W_out)
    x = x + _L0_ffn_ref(_layernorm(x, axis=-1), L0_ffn_routing_token, L0_ffn_light_gamma, L0_ffn_light_w1, L0_ffn_light_b1, L0_ffn_light_w2, L0_ffn_light_b2, L0_ffn_heavy_gamma, L0_ffn_heavy_w1, L0_ffn_heavy_b1, L0_ffn_heavy_w2, L0_ffn_heavy_b2)
    x = x + _L0_attn_b_ref(_layernorm(x, axis=-1), L0_attn_b_Wq, L0_attn_b_Wk, L0_attn_b_Wv)
    x = x + _L0_ffn_ref(_layernorm(x, axis=-1), L0_ffn_routing_token, L0_ffn_light_gamma, L0_ffn_light_w1, L0_ffn_light_b1, L0_ffn_light_w2, L0_ffn_light_b2, L0_ffn_heavy_gamma, L0_ffn_heavy_w1, L0_ffn_heavy_b1, L0_ffn_heavy_w2, L0_ffn_heavy_b2)
    return x

_drawn_inputs = setup_inputs


def setup_inputs(seed=0):
    import zlib

    import numpy as np

    out = dict(_drawn_inputs(seed))
    spreads = {'L0_attn_a_b_beta': (2.0, 0.2),
     'L0_ffn_light_gamma': (1.0, 0.2),
     'L0_ffn_light_b1': (0.0, 0.1),
     'L0_ffn_light_b2': (0.0, 0.1),
     'L0_ffn_heavy_gamma': (1.0, 0.6),
     'L0_ffn_heavy_b1': (0.0, 0.358),
     'L0_ffn_heavy_b2': (0.0, 0.1)}
    factors = {}
    for name, (base, spread) in spreads.items():
        noise = np.random.default_rng([zlib.crc32(name.encode()), seed]).standard_normal(out[name].shape)
        drawn = base * np.exp(spread * noise) if base else spread * noise
        out[name] = jnp.asarray(drawn.astype(out[name].dtype))
    for name, factor in factors.items():
        out[name] = (out[name] * factor).astype(out[name].dtype)
    return out
```

```python
import math
from contextlib import ExitStack
import concourse.bass as bass
from concourse import mybir

F32 = mybir.dt.float32
BF16 = mybir.dt.bfloat16
ALU = mybir.AluOpType
ACT = mybir.ActivationFunctionType
AX_X = mybir.AxisListType.X
P = 128
NB = 32
NH = 8
N = 32
TB = 32
U = 8
POOL_C = 24


def phase_semaphores(nc, ctx, prefix):
    own = []

    def clear():
        nc.all_engine_barrier()
        nc.clear_and_free_semaphores(own)
        nc.all_engine_barrier()

    def sem(name):
        own.append(nc.alloc_semaphore(name=prefix + name))
        return own[-1]

    ctx.callback(clear)
    return sem


def make_identity(nc, ident, made, ready):
    nc.gpsimd.memset(ident[:], 0.0).then_inc(made, 1)
    nc.gpsimd.wait_ge(made, 1)
    nc.gpsimd.affine_select(out=ident[:], in_=ident[:], compare_op=ALU.not_equal, fill=1.0, base=0,
                            pattern=[[-1, P]], channel_multiplier=1).then_inc(ready, 1)


def scan_phase(nc, kT, qT, vbR, cell, T):
    CH, SETS = T // TB, T // U
    with ExitStack() as ctx:
        sb = lambda n, s, d=F32: ctx.enter_context(nc.sbuf_tensor(n, s, d))
        ps = lambda n, s: ctx.enter_context(nc.psum_tensor(n, s, F32))
        sem = phase_semaphores(nc, ctx, "c")
        state = sb("state", [P, 2, 1024])
        scaled = sb("scaled", [P, 2, 1024])
        kprod = sb("kprod", [P, 2, 1024])
        qprod = sb("qprod", [P, 2, 1024])
        blocks = sb("blocks", [P, P])
        spread = sb("spread", [12, P], BF16)
        pick = sb("pick", [P, U, 32])
        kbuf = sb("kbuf", [P, 2, 64, TB])
        qbuf = sb("qbuf", [P, 2, 64, TB])
        qlast = sb("qlast", [P, 64, 1])
        rows = sb("rows", [12, 2, 4, 2, 2048], BF16)
        outs = sb("outs", [P, 512])
        diff = ps("diff", [P, 2, 1024])
        beta = ps("beta", [P, 1024])
        sums = ps("sums", [P, 512])

        ones_made, blocks_made, spread_made, pick_made, pick_ready = map(
            sem, ("s_ones", "s_blocks", "s_spread", "s_pick", "s_pickr"))
        state_ready = [sem(f"s_state{u}") for u in (0, 1)]
        kprod_pool = [sem(f"s_kpp{u}") for u in (0, 1)]
        kprod_dve = [sem(f"s_kpd{u}") for u in (0, 1)]
        qprod_ready = [sem(f"s_qp{u}") for u in (0, 1)]
        diff_ready = [sem(f"s_diff{u}") for u in (0, 1)]
        beta_ready, scaled_ready = sem("s_beta"), sem("s_scaled")
        outer_ready = [sem(f"s_outer{u}") for u in (0, 1)]
        sum_ready = [sem(f"s_sum{u}") for u in (0, 1)]
        qsum_done, outs_copied = sem("s_qsum"), sem("s_outs")
        sp_passed = sem("s_sppass")
        stored, last_loaded = sem("s_stored"), sem("s_qlast")
        loaded = [sem(f"s_load{r}") for r in (0, 1)]
        rows_loaded = [sem(f"s_rows{r}") for r in (0, 1)]
        LOADS = 16 * 2

        def steps(eng, body, chunk_start=None):
            with eng.Fori(0, CH // 2) as pair:
                for r in (0, 1):
                    with eng.Fori(0, TB // U) as k:
                        n = (pair * 2 + r) * (TB // U) + k
                        for e in range(U):
                            if e == 0 and chunk_start:
                                chunk_start(pair, r)
                            body(n * U + e, r, k * U + e, e, n)

        block = ctx.enter_context(nc.Block())

        @block.sync
        def _(sp):
            def load(c, r):
                now = bass.ds(c * TB, TB)
                sp.dma_start(kbuf[:, r], kT[:, :, now]).then_inc(loaded[r], 16)
                sp.dma_start(qbuf[:, r], qT[:, :, now]).then_inc(loaded[r], 16)

            def load_rows(m, r):
                sp.dma_start(rows[:, r], vbR[bass.ds(m * 4, 4)].rearrange("t k x c -> k t (x c)")
                             ).then_inc(rows_loaded[r], 16)

            def sets(n0, n1, ahead=True):
                with sp.Fori(n0, n1) as n:
                    for r in (0, 1):
                        sp.wait_ge(diff_ready[1], n * U + 4 * r + 4)
                        if ahead:
                            load_rows(n * 2 + 2 + r, r)

            load_rows(0, 0)
            load_rows(1, 1)
            load(0, 0)
            load(1, 1)
            with nc.allow_non_contiguous_dma(reason="one column"):
                sp.dma_start(qlast[:], qT[:, :, T:T + 1]).then_inc(last_loaded, 16)
            K = TB // U
            with sp.Fori(0, CH // 2 - 1) as pair:
                for r in (0, 1):
                    sets((pair * 2 + r) * K, (pair * 2 + r) * K + K)
                    sp.wait_ge(sum_ready[1], (pair * 2 + r) * TB + TB + 1)
                    sp.sem_inc(sp_passed, 1)
                    sp.wait_ge(qprod_ready[1], (pair * 2 + r) * TB + TB)
                    load(pair * 2 + r + 2, r)
            sets((CH - 2) * K, SETS - 1)

        @block.gpsimd
        def _(pool):
            nc.gpsimd.memset(blocks[:], -1.0).then_inc(ones_made, 1)
            pool.wait_ge(ones_made, 1)
            v = blocks[:].rearrange("p (q j) -> p q j", q=4)
            nc.gpsimd.affine_select(out=v, in_=v, compare_op=ALU.is_ge, fill=0.0, base=0,
                                    pattern=[[-32, 4], [0, 32]], channel_multiplier=1).then_inc(ones_made, 1)
            pool.wait_ge(ones_made, 2)
            nc.gpsimd.affine_select(out=v, in_=v, compare_op=ALU.is_ge, fill=0.0, base=31,
                                    pattern=[[32, 4], [0, 32]], channel_multiplier=-1).then_inc(blocks_made, 1)
            nc.gpsimd.memset(spread[:], 0.0).then_inc(spread_made, 1)
            for s in range(3):
                pool.wait_ge(spread_made, s + 1)
                v = spread[:].rearrange("k (q j) -> k q j", q=4)
                nc.gpsimd.affine_select(out=v, in_=v, compare_op=ALU.not_equal, fill=1.0, base=-4 * s,
                                        pattern=[[-1, 4], [0, 32]], channel_multiplier=1).then_inc(spread_made, 1)
            nc.gpsimd.memset(pick[:].rearrange("p e m -> p (e m)"), 0.0).then_inc(pick_made, 1)
            pool.wait_ge(blocks_made, 1)
            pool.wait_ge(pick_made, 1)
            for e in range(U):
                nc.gpsimd.tensor_scalar(pick[:, e, 4 * e:4 * e + 4], blocks[:, 0:P:32], -1.0, None, ALU.mult
                                        ).then_inc(pick_ready, 1)

            def arrived(pair, r):
                pool.wait_ge(loaded[r], pair * LOADS + LOADS)

            def step(t, r, tt, e, n):
                cols = lambda x, u, m: x[:, u, 0:N * m].rearrange("p (c i) -> p c i", i=N)
                for u in (0, 1):
                    pool.wait_ge(state_ready[u], t + 1)
                    if POOL_C:
                        nc.gpsimd.tensor_tensor(cols(kprod, u, POOL_C), cols(state, u, POOL_C),
                                                kbuf[:, r, 32 * u:32 * u + POOL_C, bass.ds(tt, 1)].to_broadcast([P, POOL_C, N]),
                                                ALU.mult).then_inc(kprod_pool[u], 1)
                for u in (0, 1):
                    pool.wait_ge(qsum_done, t * 2 + u + 1)
                    nc.gpsimd.tensor_tensor(cols(qprod, u, 32), cols(state, u, 32),
                                            qbuf[:, r, 32 * u:32 * u + 32, bass.ds(tt, 1)].to_broadcast([P, 32, N]),
                                            ALU.mult).then_inc(qprod_ready[u], 1)

            steps(pool, step, arrived)
            pool.wait_ge(last_loaded, 16)
            for u in (0, 1):
                pool.wait_ge(state_ready[u], T + 1)
                pool.wait_ge(qsum_done, T * 2 + u + 1)
                nc.gpsimd.tensor_tensor(qprod[:, u].rearrange("p (c i) -> p c i", i=N), state[:, u].rearrange("p (c i) -> p c i", i=N),
                                        qlast[:, 32 * u:32 * u + 32].to_broadcast([P, 32, N]), ALU.mult
                                        ).then_inc(qprod_ready[u], 1)

        @block.tensor
        def _(pe):
            pe.sem_inc(qsum_done, 2)
            pe.wait_ge(blocks_made, 1)
            pe.wait_ge(spread_made, 4)
            pe.wait_ge(pick_ready, U)

            def step(t, r, tt, e, n):
                if e % 4 == 0:
                    pe.wait_ge(rows_loaded[e // 4], n * 16 + 16)
                for u in (0, 1):
                    pe.wait_ge(scaled_ready, t * 2 + u + 1)
                    for w in (0, 1):
                        c = 1024 * u + 512 * w
                        mm = nc.tensor.matmul(beta[:, 512 * w:512 * w + 512], spread[:],
                                              rows[:, e // 4, e % 4, 1, c:c + 512], start=True, stop=True)
                    mm.then_inc(beta_ready, 1)
                    pe.wait_ge(state_ready[u], t + 1)
                    for w in (0, 1):
                        c = 1024 * u + 512 * w
                        nc.tensor.matmul(diff[:, u, 512 * w:512 * w + 512], spread[:],
                                         rows[:, e // 4, e % 4, 0, c:c + 512], start=True, stop=False)
                    if POOL_C:
                        pe.wait_ge(kprod_pool[u], t + 1)
                    if POOL_C < 32:
                        pe.wait_ge(kprod_dve[u], t + 1)
                    for w in (0, 1):
                        mm = nc.tensor.matmul(diff[:, u, 512 * w:512 * w + 512], blocks[:],
                                              kprod[:, u, 512 * w:512 * w + 512], start=False, stop=True)
                    mm.then_inc(diff_ready[u], 1)
                if e == 0:
                    pe.wait_ge(outs_copied, n + 1)
                qsum(t, e, e == U - 1)

            def qsum(t, e, stop):
                for u in (0, 1):
                    pe.wait_ge(qprod_ready[u], t + 1)
                    for w in (0, 1):
                        z = 2 * u + w
                        mm = nc.tensor.matmul(sums[32 * z:32 * z + 32, :], pick[:, e], qprod[:, u, 512 * w:512 * w + 512],
                                              start=(e == 0), stop=stop, skip_group_check=True)
                    mm.then_inc(qsum_done, 1)

            steps(pe, step)
            pe.wait_ge(outs_copied, SETS + 1)
            qsum(T, 0, True)

        @block.vector
        def _(dve):
            for u in (0, 1):
                nc.vector.memset(state[:, u], 0.0).then_inc(state_ready[u], 1)
                dve.sem_inc(sum_ready[u], 1)
            dve.sem_inc(scaled_ready, 1)

            def arrived(pair, r):
                dve.wait_ge(loaded[r], pair * LOADS + LOADS)

            def step(t, r, tt, e, n):
                for u in (0, 1):
                    dve.wait_ge(state_ready[u], t + 1)
                    if POOL_C < 32:
                        D = 32 - POOL_C
                        cols = lambda x: x[:, u, N * POOL_C:].rearrange("p (c i) -> p c i", i=N)
                        nc.vector.tensor_tensor(cols(kprod), cols(state),
                                                kbuf[:, r, 32 * u + POOL_C:32 * u + 32, bass.ds(tt, 1)].to_broadcast([P, D, N]),
                                                ALU.mult).then_inc(kprod_dve[u], 1)
                for u in (0, 1):
                    dve.wait_ge(beta_ready, t * 2 + u + 1)
                    nc.vector.tensor_tensor(scaled[:, u], beta[:], state[:, u], ALU.mult).then_inc(scaled_ready, 1)
                for u in (0, 1):
                    dve.wait_ge(diff_ready[u], t + 1)
                    o = diff[:, u].rearrange("p (c i) -> p c i", i=N)
                    nc.vector.tensor_tensor(o, o, kbuf[:, r, 32 * u:32 * u + 32, bass.ds(tt, 1)].to_broadcast([P, 32, N]),
                                            ALU.mult).then_inc(outer_ready[u], 1)
                    dve.wait_ge(outer_ready[u], t + 1)
                    dve.wait_ge(scaled_ready, t * 2 + u + 2)
                    nc.vector.tensor_tensor(diff[:, u], diff[:, u], scaled[:, u], ALU.add).then_inc(sum_ready[u], 1)

            steps(dve, step, arrived)

        @block.scalar
        def _(act):
            act.sem_inc(outs_copied, 1)

            act.sem_inc(stored, 64)

            def put_out(n, t):
                act.wait_ge(qsum_done, t * 2 + 4)
                act.wait_ge(stored, n * 64 + 64)
                nc.scalar.copy(outs[:], sums[:]).then_inc(outs_copied, 1)
                act.wait_ge(outs_copied, n + 2)
                for z in range(4):
                    act.dma_start(cell[bass.ds(n * U, U), z], outs[32 * z:32 * z + 32]).then_inc(stored, 16)

            def step(t, r, tt, e, n):
                for u in (0, 1):
                    act.wait_ge(sum_ready[u], t + 2)
                    act.wait_ge(qprod_ready[u], t + 1)
                    nc.scalar.activation(state[:, u], diff[:, u], ACT.Tanh).then_inc(state_ready[u], 1)
                if e == U - 1:
                    put_out(n, t)

            steps(act, step)
            put_out(SETS, T)
            act.wait_ge(stored, SETS * 64 + 128)


def done(n, k=1, per=1):
    return n * per + k + per


def credit(eng, sems):
    for s, per in sems:
        eng.sem_inc(s, per)


def turn_weights(nc, block, jobs, stage, ps, ident, ident_ready, sem):
    w_loaded = [sem(f"s_wload{e}") for e in (0, 1)]
    w_turned, w_put = sem("s_wturn"), sem("s_wput")
    J = len(jobs)

    def loads(sp):
        for j, (w, _) in enumerate(jobs):
            if j >= 2:
                sp.wait_ge(w_turned, j - 1)
            R = w.shape[0] // P
            sp.dma_start(stage[:, j % 2, 0:R], w.rearrange("(r p) e -> p r e", p=P)).then_inc(w_loaded[j % 2], 16)

    def turns(pe):
        pe.wait_ge(ident_ready, 1)
        for j, (w, _) in enumerate(jobs):
            R = w.shape[0] // P
            pe.wait_ge(w_loaded[j % 2], 16 * (j // 2 + 1))
            if j >= 2:
                pe.wait_ge(w_put, j - 1)
            for r in range(R):
                for k in range(2):
                    mm = nc.tensor.transpose(ps[:, j % 2, (2 * r + k) * P:(2 * r + k + 1) * P], stage[:, j % 2, r, k * P:k * P + P], ident[:])
            mm.then_inc(w_turned, 1)

    def puts(dve):
        for j, (w, target) in enumerate(jobs):
            R = w.shape[0] // P
            dve.wait_ge(w_turned, j + 1)
            for r in range(R):
                for k in range(2):
                    src = ps[:, j % 2, (2 * r + k) * P:(2 * r + k + 1) * P]
                    dst = target(k, r)
                    if len(dst.shape) == 3:
                        src = src.rearrange("p (q i) -> p q i", q=4)
                    last = nc.vector.tensor_copy(dst, src)
            last.then_inc(w_put, 1)

    return loads, turns, puts, w_put


def project_phase(nc, x, W_in, W_k, W_v, W_q, W_beta, b_beta, kT, qT, vbR, T):
    TT = T // P
    EPS = 1e-5
    with ExitStack() as ctx:
        sb = lambda n, s, d=F32: ctx.enter_context(nc.sbuf_tensor(n, s, d))
        ps = lambda n, s: ctx.enter_context(nc.psum_tensor(n, s, F32))
        sem = phase_semaphores(nc, ctx, "p")
        ident = sb("p_ident", [P, P])
        w_stage = sb("w_stage", [P, 2, 2, 256])
        w_in = sb("w_in", [P, 2, 256])
        w_k = sb("w_k", [P, 2, 256])
        w_q = sb("w_q", [P, 2, 256])
        w_vb = sb("w_vb", [P, 2, 2, 4, 2, 32])
        bias = sb("bias", [P, 4, 2, 32])
        eps = sb("eps", [P, 1])
        xt = sb("xt", [P, 2, 4, 256])
        stats = sb("stats", [P, 4, 6])
        mv = sb("mv", [P, 4, 2])
        std = sb("std", [P, 4])
        rstd = sb("rstd", [P, 4])
        xn = sb("xn", [P, 4, 256])
        xnT = sb("xnT", [P, 2, 512])
        sig = sb("sig", [P, 2, 512])
        xp = sb("xp", [P, 2, 512])
        ksq = sb("ksq", [P, 4, 256])
        ksum = sb("ksum", [P, 32])
        knorm = sb("knorm", [P, 32])
        kinv = sb("kinv", [P, 32])
        kn = sb("kn", [P, 4, 256])
        k_out = sb("k_out", [P, 8, P])
        q_out = sb("q_out", [P, 8, P])
        vb = sb("vb", [P, 4, 2, 4, 64])
        parts = sb("parts", [P, 3, 2048], BF16)
        rest = sb("rest", [P, 2, 2048])
        zero = sb("zero", [P, 64, 1])
        turned = ps("p_turned", [P, 2, 512])
        xpp = ps("p_xp", [P, 2, 512])
        kk = ps("p_k", [P, 4, 256])
        vbp = ps("p_vb", [P, 2, 512])

        ident_zero, ident_ready, eps_ready, zero_ready, zero_stored, bias_loaded = map(
            sem, ("s_id0", "s_id1", "s_eps", "s_zero", "s_zst", "s_bias"))
        x_loaded = [sem(f"s_x{e}") for e in (0, 1)]
        stats_done, aggr_done, std_done, rstd_done, xn_done, x_turned, xnT_done, xpp_done = map(
            sem, ("s_st", "s_ag", "s_std", "s_rstd", "s_xn", "s_xt", "s_xnT", "s_xpp"))
        sig_done, xp_done, k_done, q_done, ksq_done, ksum_done, knorm_done, keps_done, kinv_done, kn_done, k_turned = map(
            sem, ("s_sig", "s_xp", "s_k", "s_q", "s_ksq", "s_ksum", "s_knorm", "s_keps", "s_kinv", "s_kn", "s_kt"))
        k_put, q_put, vb_done, v_put, b_put, b_sig = map(sem, ("s_kput", "s_qput", "s_vb", "s_vput", "s_bput", "s_bsig"))
        part1, rest1, part2, part3 = map(sem, ("s_part1", "s_rest1", "s_part2", "s_part3"))
        dve_passed, pool_passed = sem("s_dpass"), sem("s_ppass")
        k_stored, q_stored, vb_stored = map(sem, ("s_kst", "s_qst", "s_vbst"))

        jobs = [(W_in, lambda k, r: w_in[:, k, r * P:r * P + P]),
                (W_k, lambda k, r: w_k[:, k, r * P:r * P + P]),
                (W_q, lambda k, r: w_q[:, k, r * P:r * P + P]),
                (W_v, lambda k, r: w_vb[:, k, 0, :, r, :]),
                (W_beta, lambda k, r: w_vb[:, k, 1, :, r, :])]
        block = ctx.enter_context(nc.Block())
        loads, turns, puts, w_put = turn_weights(nc, block, jobs, w_stage, turned, ident, ident_ready, sem)

        def tiles(eng, body):
            with eng.Fori(0, NB // 4 * TT // 2) as m:
                for e in (0, 1):
                    body(m * 2 + e, e)

        @block.sync
        def _(sp):
            loads(sp)
            with nc.allow_non_contiguous_dma(reason="rows of 128 bytes"):
                for f in range(2):
                    src = b_beta.rearrange("(f q) i -> f q i", f=2)[f]
                    sp.dma_start(bias[:, :, f], src.partition_broadcast(P)).then_inc(bias_loaded, 16)
            sp.wait_ge(zero_ready, 1)
            with nc.allow_non_contiguous_dma(reason="one column"):
                sp.dma_start(qT[:, :, 0:1], zero[:]).then_inc(zero_stored, 16)

            def load(n, e):
                sp.wait_ge(xn_done, done(n, 0, 4))
                sp.dma_start(xt[:, e], x[bass.ds(n // TT * 4, 4), bass.ds(n % TT * P, P), :].rearrange("b t d -> t b d")
                             ).then_inc(x_loaded[e], 16)

            def store(n):
                B, tt = n // TT, n % TT
                sp.wait_ge(q_put, done(n, 1))
                sp.dma_start(qT[:, bass.ds(B * 8, 8), bass.ds(tt * P + 1, P)], q_out[:]).then_inc(q_stored, 16)
                sp.wait_ge(k_put, done(n, 1))
                sp.dma_start(kT[:, bass.ds(B * 8, 8), bass.ds(tt * P, P)], k_out[:]).then_inc(k_stored, 16)
                sp.wait_ge(part3, done(n, 1))
                sp.dma_start(vbR[bass.ds(tt * P, P), :, :, bass.ds(B * 256, 256)].rearrange("t k x c -> t (k x) c"),
                             parts[:].rearrange("p s (m c) -> p (s m) c", c=256)).then_inc(vb_stored, 16)

            TILES = NB // 4 * TT
            credit(sp, [(k_stored, 16), (q_stored, 16), (vb_stored, 16)])
            load(0, 0)
            with sp.Fori(0, TILES // 2 - 1) as m:
                for e in (0, 1):
                    load(m * 2 + 1 + e, 1 - e)
                    store(m * 2 + e)
            load(TILES - 1, 1)
            store(TILES - 2)
            store(TILES - 1)
            for s in (k_stored, q_stored, vb_stored):
                sp.wait_ge(s, 16 * (TILES + 1))
            sp.wait_ge(zero_stored, 16)

        @block.gpsimd
        def _(pool):
            make_identity(nc, ident, ident_zero, ident_ready)
            nc.gpsimd.memset(zero[:], 0.0).then_inc(zero_ready, 1)
            credit(pool, [(part1, 1), (part2, 1)])

            def tile(n, e):
                pool.wait_ge(v_put, done(n, 4, 4))
                pool.wait_ge(b_sig, done(n, 1))
                pool.wait_ge(vb_stored, done(n, 0, 16))
                pool.sem_inc(pool_passed, 1)
                nc.gpsimd.tensor_copy(parts[:, 0], vb[:].rearrange("p q x b c -> p (q x b c)")).then_inc(part1, 1)
                pool.wait_ge(rest1, done(n, 1))
                pool.sem_inc(pool_passed, 1)
                nc.gpsimd.tensor_copy(parts[:, 1], rest[:, 0]).then_inc(part2, 1)

            tiles(pool, tile)
        @block.tensor
        def _(pe):
            turns(pe)
            pe.wait_ge(w_put, len(jobs))
            credit(pe, [(x_turned, 1), (xpp_done, 1), (k_done, 1), (q_done, 1), (vb_done, 2), (k_turned, 1)])

            def tile(n, e):
                pe.wait_ge(xn_done, done(n, 4, 4) + 4)
                pe.wait_ge(q_put, done(n, 0))
                for b in range(4):
                    for k in range(2):
                        mm = nc.tensor.transpose(turned[:, k, b * P:b * P + P], xn[:, b, k * P:k * P + P], ident[:])
                mm.then_inc(x_turned, 1)
                pe.wait_ge(xnT_done, done(n, 1))
                pe.wait_ge(k_put, done(n, 0))
                for c in range(2):
                    for k in range(2):
                        mm = nc.tensor.matmul(xpp[:, c], w_in[:, k, c * P:c * P + P], xnT[:, k], start=(k == 0), stop=(k == 1))
                mm.then_inc(xpp_done, 1)
                pe.wait_ge(xp_done, done(n, 1))
                pe.wait_ge(kn_done, done(n, 0))
                for b in range(4):
                    for k in range(2):
                        mm = nc.tensor.matmul(kk[:, b], xp[:, k, b * P:b * P + P], w_k[:, k], start=(k == 0), stop=(k == 1))
                mm.then_inc(k_done, 1)
                for h in range(2):
                    pe.wait_ge(v_put, done(n, 2 * h, 4))
                    pe.wait_ge(b_put, done(n, 2 * h, 4))
                    for b in (2 * h, 2 * h + 1):
                        for k in range(2):
                            mm = nc.tensor.matmul(vbp[:, b % 2], xp[:, k, b * P:b * P + P],
                                                  w_vb[:, k].rearrange("p x q f i -> p (x q f i)"), start=(k == 0), stop=(k == 1))
                    mm.then_inc(vb_done, 1)
                    if h == 0:
                        for f in range(2):
                            for k in range(2):
                                mm = nc.tensor.matmul(turned[:, f], w_q[:, k, f * P:f * P + P], xp[:, k], start=(k == 0), stop=(k == 1))
                        mm.then_inc(q_done, 1)
                pe.wait_ge(kn_done, done(n, 1))
                for b in range(4):
                    for f in range(2):
                        mm = nc.tensor.transpose(xpp[:, f, b * P:b * P + P], kn[:, b, f * P:f * P + P], ident[:])
                mm.then_inc(k_turned, 1)

            tiles(pe, tile)

        @block.vector
        def _(dve):
            nc.vector.memset(eps[:], EPS).then_inc(eps_ready, 1)
            puts(dve)
            credit(dve, [(stats_done, 4), (aggr_done, 4), (rstd_done, 1), (xn_done, 8), (xnT_done, 1), (xp_done, 1), (ksum_done, 1),
                         (keps_done, 1), (kinv_done, 1), (kn_done, 1), (k_put, 1), (b_put, 4), (rest1, 1), (part3, 1)])
            dve.wait_ge(bias_loaded, 32)

            def tile(n, e):
                dve.wait_ge(x_loaded[e], (n - e) * 8 + 16)
                for b in range(4):
                    nc.vector.bn_stats(stats[:, b], xt[:, e, b]).then_inc(stats_done, 1)
                for b in range(4):
                    dve.wait_ge(stats_done, done(n, b + 1, 4))
                    dve.sem_inc(dve_passed, 1)
                    nc.vector.bn_aggr(mv[:, b], stats[:, b]).then_inc(aggr_done, 1)
                dve.wait_ge(std_done, done(n, 1))
                nc.vector.reciprocal(rstd[:], std[:]).then_inc(rstd_done, 1)
                dve.wait_ge(rstd_done, done(n, 1))
                dve.wait_ge(x_turned, done(n, 0))
                for b in range(4):
                    nc.vector.tensor_scalar(xn[:, b], xt[:, e, b], mv[:, b, 0:1], rstd[:, b:b + 1], ALU.subtract, ALU.mult
                                            ).then_inc(xn_done, 1)
                dve.wait_ge(x_turned, done(n, 1))
                nc.vector.tensor_copy(xnT[:], turned[:]).then_inc(xnT_done, 1)
                dve.wait_ge(sig_done, done(n, 1))
                nc.vector.tensor_tensor(xp[:], xpp[:], sig[:], ALU.mult).then_inc(xp_done, 1)
                dve.wait_ge(ksq_done, done(n, 1))
                nc.vector.tensor_reduce(ksum[:], ksq[:].rearrange("p b (h j) -> p (b h) j", j=N), AX_X, ALU.add).then_inc(ksum_done, 1)
                for b in range(4):
                    dve.wait_ge(vb_done, done(n, b // 2 + 1, 2))
                    if b == 0:
                        dve.wait_ge(part3, done(n, 0))
                        dve.wait_ge(part1, done(n, 0))
                    nc.vector.tensor_tensor(vb[:, :, 1, b], vbp[:, b % 2, 256:512].rearrange("p (q c) -> p q c", q=4),
                                            bias[:].rearrange("p q f i -> p q (f i)"), ALU.add).then_inc(b_put, 1)
                dve.wait_ge(knorm_done, done(n, 1))
                nc.vector.tensor_scalar(knorm[:], knorm[:], 1e-6, None, ALU.add).then_inc(keps_done, 1)
                dve.wait_ge(keps_done, done(n, 1))
                nc.vector.reciprocal(kinv[:], knorm[:]).then_inc(kinv_done, 1)
                dve.wait_ge(kinv_done, done(n, 1))
                nc.vector.tensor_tensor(kn[:].rearrange("p b (h j) -> p (b h) j", j=N), kk[:].rearrange("p b (h j) -> p (b h) j", j=N),
                                        kinv[:].unsqueeze(2).to_broadcast([P, 32, N]), ALU.mult).then_inc(kn_done, 1)
                dve.wait_ge(part1, done(n, 1))
                flat = vb[:].rearrange("p q x b c -> p (q x b c)")
                nc.vector.tensor_tensor(rest[:, 0], flat, parts[:, 0], ALU.subtract).then_inc(rest1, 1)
                dve.wait_ge(k_turned, done(n, 1))
                dve.wait_ge(k_stored, done(n, 0, 16))
                nc.vector.tensor_copy(k_out[:].rearrange("p (b f) t -> p f b t", f=2),
                                      xpp[:].rearrange("p f (b t) -> p f b t", b=4)).then_inc(k_put, 1)
                dve.wait_ge(part2, done(n, 1))
                nc.vector.tensor_tensor(parts[:, 2], rest[:, 0], parts[:, 1], ALU.subtract).then_inc(part3, 1)

            tiles(dve, tile)

        @block.scalar
        def _(act):
            credit(act, [(std_done, 1), (sig_done, 1), (ksq_done, 1), (knorm_done, 1), (q_put, 1), (v_put, 4), (b_sig, 1)])
            act.wait_ge(eps_ready, 1)

            def tile(n, e):
                act.wait_ge(aggr_done, done(n, 4, 4))
                act.wait_ge(rstd_done, done(n, 0))
                nc.scalar.activation(std[:], mv[:, :, 1], ACT.Sqrt, bias=eps[:]).then_inc(std_done, 1)
                act.wait_ge(xpp_done, done(n, 1))
                act.wait_ge(xp_done, done(n, 0))
                nc.scalar.activation(sig[:], xpp[:], ACT.Sigmoid).then_inc(sig_done, 1)
                act.wait_ge(k_done, done(n, 1))
                act.wait_ge(ksum_done, done(n, 0))
                nc.scalar.activation(ksq[:], kk[:], ACT.Square).then_inc(ksq_done, 1)
                for b in range(4):
                    act.wait_ge(vb_done, done(n, b // 2 + 1, 2))
                    act.wait_ge(b_put, done(n, 2 * (b // 2) + 2, 4))
                    if b == 0:
                        act.wait_ge(part3, done(n, 0))
                        act.wait_ge(part1, done(n, 0))
                    nc.scalar.copy(vb[:, :, 0, b], vbp[:, b % 2, 0:256].rearrange("p (q c) -> p q c", q=4)).then_inc(v_put, 1)
                    if b == 1:
                        act.wait_ge(q_done, done(n, 1))
                        act.wait_ge(q_stored, done(n, 0, 16))
                        nc.scalar.copy(q_out[:].rearrange("p (b f) t -> p f b t", f=2),
                                       turned[:].rearrange("p f (b t) -> p f b t", b=4)).then_inc(q_put, 1)
                beta = vb[:, :, 1].rearrange("p q b c -> p q (b c)")
                nc.scalar.activation(beta, beta, ACT.Sigmoid).then_inc(b_sig, 1)
                act.wait_ge(ksum_done, done(n, 1))
                act.wait_ge(kinv_done, done(n, 0))
                nc.scalar.activation(knorm[:], ksum[:], ACT.Sqrt).then_inc(knorm_done, 1)

            tiles(act, tile)


D = 256
LN_EPS = 1e-5
SLOTS = 256


def done2(n, k=1):
    return n + k + 2


def light_phase(nc, tag, xin, cell, W_out, gamma, w1, b1, w2, b2, token, x2, xr_rows, s_rows):
    T = 512
    with ExitStack() as ctx:
        sb = lambda n, s, d=F32: ctx.enter_context(nc.sbuf_tensor(tag + n, s, d))
        ps = lambda n, s: ctx.enter_context(nc.psum_tensor(tag + n, s, F32))
        sem = phase_semaphores(nc, ctx, tag + "s_")
        ident = sb("ident", [P, P])
        wo_stage = sb("wo_stage", [P, 2, 256])
        wo = sb("wo", [P, 2, 256])
        w1_raw = sb("w1_raw", [P, 2, 128])
        w1g = sb("w1g", [P, 2, 128])
        gam = sb("gam", [P, 2])
        b1c = sb("b1c", [P, 1])
        w2s = sb("w2s", [P, 256])
        b2r = sb("b2r", [P, 256])
        tok = sb("tok", [P, 256])
        eps = sb("eps", [P, 1])
        xt = sb("xt", [P, 2, 4, 256])
        ot = sb("ot", [P, 2, 4, 256])
        sig = sb("sig", [P, 4, 256])
        osq = sb("osq", [P, 4, 256])
        oo = sb("oo", [P, 4, 256])
        oT = sb("oT", [P, 2, 512])
        stats = sb("stats", [P, 4, 6])
        mv = sb("mv", [P, 4, 2])
        std = sb("std", [P, 2, 4])
        rstd = sb("rstd", [P, 4])
        norm = sb("norm", [P, 4])
        normc = sb("normc", [P, 4])
        inv = sb("inv", [P, 4])
        inv16 = sb("inv16", [P, 4])
        rscale = sb("rscale", [P, 4])
        xr = sb("xr", [P, 2, 4, 256])
        prod = sb("prod", [P, 4, 256])
        dot = sb("dot", [P, 4])
        dotn = sb("dotn", [P, 4])
        ss = sb("ss", [P, 4, NB])
        xrT = sb("xrT", [P, 2, 512])
        hid = sb("hid", [P, 512])
        xb = sb("xb", [P, 4, 256])
        xo = sb("xo", [P, 2, 4, 256])
        s_out = sb("s_out", [NB, 512])
        pa = ps("pa", [P, 2, 512])
        pb = ps("pb", [P, 4, 256])
        pc = ps("pc", [P, 512])
        pd = ps("pd", [P, 4, 256])

        id0, id_ready, eps_ready, w_loaded, w_turned, w_put, w1_ready = map(
            sem, ("id0", "id1", "eps", "w", "wturn", "wput", "w1"))
        x_loaded = [sem(f"x{e}") for e in (0, 1)]
        o_loaded = [sem(f"o{e}") for e in (0, 1)]
        sig_done, osq_done, oo_done, o_turned, oT_done, y_done, x1_done = map(
            sem, ("sig", "osq", "oo", "oturn", "oT", "y", "xplus"))
        st_done, ag_done, std_done, r1, r2, r3, r4, r5, r6, xr_done = map(
            sem, ("st", "ag", "std", "r1", "r2", "r3", "r4", "r5", "r6", "xr"))
        prod_done, dot_done, dotn_done, ss_done, xr_turned, xrT_done, h_done, gelu_done, light_done, xb_done, x2_done = map(
            sem, ("prod", "dot", "dotn", "ss", "xrt", "xrT", "h", "gelu", "light", "xb", "x2"))
        x2_stored, xr_stored, dpass, s_turned, s_put, s_stored = map(sem, ("x2st", "xrst", "dpass", "sturn", "sput", "sst"))
        block = ctx.enter_context(nc.Block())
        WLOADS = 16 * (10 if cell is not None else 6)

        def tiles(eng, body):
            with eng.Fori(0, NB // 2) as m:
                for e in (0, 1):
                    body(m * 2 + e, e, m)

        @block.sync
        def _(sp):
            with nc.allow_non_contiguous_dma(reason="small constants"):
                sp.dma_start(w1_raw[:], w1.rearrange("(k p) m -> p k m", p=P)).then_inc(w_loaded, 16)
                sp.dma_start(gam[:], gamma.rearrange("(k p) -> p k", p=P)).then_inc(w_loaded, 16)
                sp.dma_start(b1c[:], b1.rearrange("(p o) -> p o", o=1)).then_inc(w_loaded, 16)
                sp.dma_start(w2s[:], w2).then_inc(w_loaded, 16)
                sp.dma_start(b2r[:], b2.partition_broadcast(P)).then_inc(w_loaded, 16)
                sp.dma_start(tok[:], token.partition_broadcast(P)).then_inc(w_loaded, 16)
                if cell is not None:
                    src = W_out.rearrange("(r p) (f q i) -> r f p q i", p=P, f=2, q=4)
                    for r in range(2):
                        for f in range(2):
                            dst = wo_stage[:, r].rearrange("p (q f i) -> p q f i", q=4, f=2)[:, :, f]
                            sp.dma_start(dst, src[r, f]).then_inc(w_loaded, 16)

            def load(n, e):
                sp.wait_ge(x2_done, done2(n, -1))
                sp.dma_start(xt[:, e], xin[bass.ds(n, 1)].rearrange("o (b p) d -> p (o b) d", p=P)).then_inc(x_loaded[e], 16)
                if cell is not None:
                    sp.wait_ge(oo_done, done2(n, -1))
                    for t in range(4):
                        src = cell[t * P + 1:t * P + P + 1, bass.ds(n // 8, 1), :, bass.ds(n % 8 * 64, 64)]
                        sp.dma_start(ot[:, e, t].rearrange("p (q c) -> p q c", q=4),
                                     src.rearrange("t z q c -> t (z q) c")).then_inc(o_loaded[e], 16)

            def store(n, e):
                sp.wait_ge(xr_done, done(n, 4, 4))
                sp.dma_start(xr_rows[bass.ds(n * T, T), :].rearrange("(b p) d -> p b d", p=P), xr[:, e]).then_inc(xr_stored, 16)
                sp.wait_ge(x2_done, done2(n, 1))
                sp.dma_start(x2[bass.ds(n * T, T), :].rearrange("(b p) d -> p b d", p=P), xo[:, e]).then_inc(x2_stored, 16)

            credit(sp, [(x2_stored, 32), (xr_stored, 32)])
            with nc.allow_non_contiguous_dma(reason="runs of 256 bytes"):
                load(0, 0)
                with sp.Fori(0, NB // 2 - 1) as m:
                    for e in (0, 1):
                        load(m * 2 + 1 + e, 1 - e)
                        store(m * 2 + e, e)
                load(NB - 1, 1)
                store(NB - 2, 0)
                store(NB - 1, 1)
            sp.wait_ge(s_put, 1)
            sp.dma_start(s_rows, s_out[:]).then_inc(s_stored, 16)
            sp.wait_ge(s_stored, 16)
            sp.wait_ge(x2_stored, 16 * NB + 32)
            sp.wait_ge(xr_stored, 16 * NB + 32)

        @block.gpsimd
        def _(pool):
            make_identity(nc, ident, id0, id_ready)
            pool.wait_ge(w_loaded, WLOADS)
            credit(pool, [(osq_done, 1), (prod_done, 1), (xb_done, 1)])

            def tile(n, e, m):
                if cell is not None:
                    pool.wait_ge(o_loaded[e], m * 64 + 64)
                    pool.wait_ge(oo_done, done2(n, 0))
                    nc.gpsimd.tensor_tensor(osq[:], ot[:, e], ot[:, e], ALU.mult).then_inc(osq_done, 1)
                    pool.wait_ge(x1_done, done(n, 1))
                else:
                    pool.wait_ge(x_loaded[e], m * 16 + 16)
                pool.wait_ge(x2_done, done2(n, 0))
                nc.gpsimd.tensor_tensor(xb[:], xt[:, e], b2r[:].unsqueeze(1).to_broadcast([P, 4, 256]), ALU.add).then_inc(xb_done, 1)
                pool.wait_ge(xr_done, done(n, 4, 4))
                pool.wait_ge(dot_done, done(n, 0))
                nc.gpsimd.tensor_tensor(prod[:], xr[:, e], tok[:].unsqueeze(1).to_broadcast([P, 4, 256]), ALU.mult).then_inc(prod_done, 1)

            tiles(pool, tile)

        @block.tensor
        def _(pe):
            pe.wait_ge(id_ready, 1)
            if cell is not None:
                pe.wait_ge(w_loaded, WLOADS)
                for k in range(2):
                    for r in range(2):
                        mm = nc.tensor.transpose(pa[:, k, r * P:r * P + P], wo_stage[:, r, k * P:k * P + P], ident[:])
                mm.then_inc(w_turned, 1)
                pe.wait_ge(w_put, 1)
            pe.wait_ge(w1_ready, 2)
            credit(pe, [(o_turned, 1), (y_done, 1), (xr_turned, 1), (h_done, 1), (light_done, 1)])

            def tile(n, e, m):
                pe.wait_ge(xrT_done, done(n, 0))
                if cell is not None:
                    pe.wait_ge(oo_done, done2(n, 1))
                    for t in range(4):
                        for k in range(2):
                            mm = nc.tensor.transpose(pa[:, k, t * P:t * P + P], oo[:, t, k * P:k * P + P], ident[:])
                    mm.then_inc(o_turned, 1)
                    pe.wait_ge(oT_done, done(n, 1))
                    pe.wait_ge(x1_done, done(n, 0))
                    for t in range(4):
                        for k in range(2):
                            mm = nc.tensor.matmul(pb[:, t], oT[:, k, t * P:t * P + P], wo[:, k], start=(k == 0), stop=(k == 1))
                    mm.then_inc(y_done, 1)
                pe.wait_ge(xr_done, done(n, 4, 4))
                for t in range(4):
                    for k in range(2):
                        mm = nc.tensor.transpose(pa[:, k, t * P:t * P + P], xr[:, e, t, k * P:k * P + P], ident[:])
                mm.then_inc(xr_turned, 1)
                pe.wait_ge(xrT_done, done(n, 1))
                pe.wait_ge(gelu_done, done(n, 0))
                for k in range(2):
                    mm = nc.tensor.matmul(pc[:], w1g[:, k], xrT[:, k], start=(k == 0), stop=(k == 1))
                mm.then_inc(h_done, 1)
                pe.wait_ge(gelu_done, done(n, 1))
                pe.wait_ge(x2_done, done2(n, 0))
                for t in range(4):
                    mm = nc.tensor.matmul(pd[:, t], hid[:, t * P:t * P + P], w2s[:], start=True, stop=True)
                mm.then_inc(light_done, 1)

            tiles(pe, tile)
            pe.wait_ge(ss_done, NB + 1)
            for t in range(4):
                mm = nc.tensor.transpose(pc[0:NB, t * P:t * P + P], ss[:, t], ident[:])
            mm.then_inc(s_turned, 1)

        @block.vector
        def _(dve):
            nc.vector.memset(eps[:], LN_EPS).then_inc(eps_ready, 1)
            dve.wait_ge(w_loaded, WLOADS)
            for k in range(2):
                nc.vector.tensor_scalar(w1g[:, k], w1_raw[:, k], gam[:, k:k + 1], None, ALU.mult).then_inc(w1_ready, 1)
            if cell is not None:
                dve.wait_ge(w_turned, 1)
                nc.vector.tensor_copy(wo[:], pa[:, :, 0:256]).then_inc(w_put, 1)
            credit(dve, [(oo_done, 2), (x1_done, 1), (st_done, 4), (ag_done, 4), (r1, 1), (r2, 1), (r3, 1), (r4, 1), (r5, 1), (r6, 1),
                         (xr_done, 4), (dot_done, 1), (dotn_done, 1), (ss_done, 1), (x2_done, 2)])

            def tile(n, e, m):
                if cell is not None:
                    dve.wait_ge(sig_done, done(n, 1))
                    dve.wait_ge(osq_done, done(n, 1))
                    dve.wait_ge(o_turned, done(n, 0))
                    nc.vector.tensor_tensor(oo[:], osq[:], sig[:], ALU.mult).then_inc(oo_done, 1)
                dve.wait_ge(x_loaded[e], m * 16 + 16)
                if cell is not None:
                    dve.wait_ge(y_done, done(n, 1))
                    nc.vector.tensor_tensor(xt[:, e], xt[:, e], pb[:], ALU.add).then_inc(x1_done, 1)
                    dve.wait_ge(x1_done, done(n, 1))
                for t in range(4):
                    nc.vector.bn_stats(stats[:, t], xt[:, e, t]).then_inc(st_done, 1)
                for t in range(4):
                    dve.wait_ge(st_done, done(n, t + 1, 4))
                    dve.sem_inc(dpass, 1)
                    nc.vector.bn_aggr(mv[:, t], stats[:, t]).then_inc(ag_done, 1)
                dve.wait_ge(std_done, done(n, 2, 2))
                nc.vector.reciprocal(rstd[:], std[:, 1]).then_inc(r1, 1)
                dve.wait_ge(r1, done(n, 1))
                nc.vector.tensor_tensor(norm[:], std[:, 0], rstd[:], ALU.mult).then_inc(r2, 1)
                dve.wait_ge(r2, done(n, 1))
                nc.vector.tensor_scalar(normc[:], norm[:], 16.0, 1e-12, ALU.mult, ALU.max).then_inc(r3, 1)
                dve.wait_ge(r3, done(n, 1))
                nc.vector.reciprocal(inv[:], normc[:]).then_inc(r4, 1)
                dve.wait_ge(r4, done(n, 1))
                nc.vector.tensor_scalar(inv16[:], inv[:], 16.0, None, ALU.mult).then_inc(r5, 1)
                dve.wait_ge(r5, done(n, 1))
                nc.vector.tensor_tensor(rscale[:], inv16[:], rstd[:], ALU.mult).then_inc(r6, 1)
                dve.wait_ge(r6, done(n, 1))
                dve.wait_ge(xr_stored, n * 16 + 16)
                for t in range(4):
                    nc.vector.tensor_scalar(xr[:, e, t], xt[:, e, t], mv[:, t, 0:1], rscale[:, t:t + 1], ALU.subtract, ALU.mult
                                            ).then_inc(xr_done, 1)
                dve.wait_ge(prod_done, done(n, 1))
                nc.vector.tensor_reduce(dot[:], prod[:], AX_X, ALU.add).then_inc(dot_done, 1)
                dve.wait_ge(dot_done, done(n, 1))
                nc.vector.tensor_tensor(dotn[:], dot[:], normc[:], ALU.mult).then_inc(dotn_done, 1)
                dve.wait_ge(dotn_done, done(n, 1))
                nc.vector.tensor_scalar(ss[:, :, bass.ds(n, 1)], dotn[:].unsqueeze(2), 1 / 16.0, None, ALU.mult).then_inc(ss_done, 1)
                dve.wait_ge(light_done, done(n, 1))
                dve.wait_ge(xb_done, done(n, 1))
                dve.wait_ge(x2_stored, n * 16 + 16)
                nc.vector.tensor_tensor(xo[:, e], xb[:], pd[:], ALU.add).then_inc(x2_done, 1)

            tiles(dve, tile)
            dve.wait_ge(s_turned, 1)
            nc.vector.tensor_copy(s_out[:], pc[0:NB, :]).then_inc(s_put, 1)

        @block.scalar
        def _(act):
            act.wait_ge(eps_ready, 1)
            act.wait_ge(w_loaded, WLOADS)
            credit(act, [(sig_done, 1), (oT_done, 1), (std_done, 2), (xrT_done, 1), (gelu_done, 1)])

            def tile(n, e, m):
                if cell is not None:
                    act.wait_ge(o_loaded[e], m * 64 + 64)
                    act.wait_ge(oo_done, done2(n, 0))
                    nc.scalar.activation(sig[:], ot[:, e], ACT.Sigmoid).then_inc(sig_done, 1)
                    act.wait_ge(o_turned, done(n, 1))
                    act.wait_ge(y_done, done(n, 0))
                    nc.scalar.copy(oT[:], pa[:]).then_inc(oT_done, 1)
                act.wait_ge(ag_done, done(n, 4, 4))
                act.wait_ge(r2, done(n, 0))
                nc.scalar.activation(std[:, 0], mv[:, :, 1], ACT.Sqrt).then_inc(std_done, 1)
                nc.scalar.activation(std[:, 1], mv[:, :, 1], ACT.Sqrt, bias=eps[:]).then_inc(std_done, 1)
                act.wait_ge(xr_turned, done(n, 1))
                act.wait_ge(h_done, done(n, 0))
                nc.scalar.copy(xrT[:], pa[:]).then_inc(xrT_done, 1)
                act.wait_ge(h_done, done(n, 1))
                act.wait_ge(light_done, done(n, 0))
                nc.scalar.activation(hid[:], pc[:], ACT.Gelu, bias=b1c[:]).then_inc(gelu_done, 1)

            tiles(act, tile)



I32 = mybir.dt.int32


def router_phase(nc, tag, s_rows, lidx, lgate):
    T, ITERS, KEEP = 512, 50, SLOTS * 9.0 / 8.0
    with ExitStack() as ctx:
        sb = lambda n, s, d=F32: ctx.enter_context(nc.sbuf_tensor(tag + n, s, d))
        ps = lambda n, s: ctx.enter_context(nc.psum_tensor(tag + n, s, F32))
        sem = phase_semaphores(nc, ctx, tag + "s_")
        ident = sb("ident", [P, P])
        s = sb("s", [NB, T])
        sb_ = sb("sb_", [NB, T])
        ex = sb("ex", [NB, T])
        smax = sb("smax", [NB, 1])
        na = sb("na", [NB, 1])
        nm = sb("nm", [NB, 1])
        tot = sb("tot", [NB, 1])
        lg = sb("lg", [NB, 1])
        z = sb("z", [NB, T])
        score = sb("score", [NB, T])
        work = sb("work", [NB, T])
        top = sb("top", [NB, 8])
        mask = sb("mask", [NB, T])
        comp = sb("comp", [NB, T])
        gate = sb("gate", [NB, T])
        upto = sb("upto", [P, P])
        ones = sb("ones", [P, P])
        slot_no = sb("slot_no", [P, SLOTS])
        maskT = sb("maskT", [P, 4, NB])
        vals = sb("vals", [P, 4, NB, 2])
        pm = sb("pm", [P, 4, NB])
        slot = sb("slot", [P, 4, NB])
        hot = sb("hot", [P, 2, 4, SLOTS])
        idx = sb("idx", [P, 2 * NB], I32)
        gates = sb("gates", [P, 2 * NB])
        pt = ps("pt", [P, 2, 4 * NB])
        pp = ps("pp", [P, 4, NB])
        pl = ps("pl", [P, NB, 2, 2])
        loaded, id0, id_ready, c_ready, made = map(sem, ("ld", "id0", "id1", "c", "made"))
        max_done, sb_done, nm_done, ex_done, ln_done, na_done, z_done, score_done = map(
            sem, ("max", "sb", "nm", "ex", "ln", "na", "z", "sc"))
        work_done, top_done, mask_done, comp_done, gate_done, turned, mT, vT, pos_done, pm_done, slot_done = map(
            sem, ("work", "top", "mask", "comp", "gate", "turn", "mT", "vT", "pos", "pm", "slot"))
        hot_done, list_done, idx_done, stored = map(sem, ("hot", "list", "idx", "st"))
        block = ctx.enter_context(nc.Block())

        @block.sync
        def _(sp):
            sp.dma_start(s[:], s_rows).then_inc(loaded, 16)
            sp.wait_ge(idx_done, 2)
            sp.dma_start(lidx, idx[:]).then_inc(stored, 16)
            sp.dma_start(lgate, gates[:]).then_inc(stored, 16)
            sp.wait_ge(stored, 32)

        @block.gpsimd
        def _(pool):
            make_identity(nc, ident, id0, id_ready)
            nc.gpsimd.memset(ones[:], 1.0).then_inc(made, 1)
            pool.wait_ge(made, 1)
            nc.gpsimd.affine_select(out=upto[:], in_=ones[:], compare_op=ALU.is_ge, fill=0.0, base=0,
                                    pattern=[[1, P]], channel_multiplier=-1).then_inc(c_ready, 1)
            nc.gpsimd.iota(slot_no[:], pattern=[[1, SLOTS]], base=0, channel_multiplier=0,
                           allow_small_or_imprecise_dtypes=True).then_inc(c_ready, 1)
            for t in range(4):
                nc.gpsimd.iota(vals[:, t, :, 0], pattern=[[T, NB]], base=t * P, channel_multiplier=1,
                               allow_small_or_imprecise_dtypes=True).then_inc(c_ready, 1)

        @block.tensor
        def _(pe):
            pe.wait_ge(id_ready, 1)
            pe.wait_ge(mask_done, 1)
            pe.wait_ge(gate_done, 1)
            for x, src in enumerate((mask, gate)):
                for t in range(4):
                    mm = nc.tensor.transpose(pt[:, x, t * NB:t * NB + NB], src[:, t * P:t * P + P], ident[0:NB, 0:NB])
            mm.then_inc(turned, 1)
            pe.wait_ge(mT, 1)
            pe.wait_ge(c_ready, 6)
            for t in range(4):
                for t2 in range(t + 1):
                    mm = nc.tensor.matmul(pp[:, t], (upto if t2 == t else ones)[:], maskT[:, t2], start=(t2 == 0), stop=(t2 == t))
            mm.then_inc(pos_done, 1)
            pe.wait_ge(vT, 1)
            pe.sem_inc(list_done, 2)
            with pe.Fori(0, NB // 2) as m:
                for e in (0, 1):
                    b = m * 2 + e
                    pe.wait_ge(hot_done, b * 4 + 4)
                    for h in range(2):
                        for t in range(4):
                            mm = nc.tensor.matmul(pl[:, bass.ds(b, 1), h, :], hot[:, e, t, h * P:h * P + P],
                                                  vals[:, t, bass.ds(b, 1), :], start=(t == 0), stop=(t == 3))
                    mm.then_inc(list_done, 1)

        @block.vector
        def _(dve):
            dve.wait_ge(loaded, 16)
            nc.vector.tensor_reduce(smax[:], s[:], AX_X, ALU.max).then_inc(max_done, 1)
            nc.vector.memset(na[:], math.log(T) - math.log(KEEP)).then_inc(na_done, 1)
            dve.wait_ge(max_done, 1)
            with dve.Fori(0, ITERS - 1) as k:
                dve.wait_ge(na_done, k + 1)
                nc.vector.tensor_scalar(nm[:], smax[:], na[:], -1.0, ALU.min, ALU.mult).then_inc(nm_done, 1)
                nc.vector.tensor_scalar(sb_[:], s[:], na[:], None, ALU.min).then_inc(sb_done, 1)
                dve.wait_ge(ln_done, k + 1)
                nc.vector.tensor_scalar(na[:], lg[:], math.log(KEEP), nm[:], ALU.subtract, ALU.subtract).then_inc(na_done, 1)
            dve.wait_ge(na_done, ITERS)
            nc.vector.tensor_scalar(z[:], s[:], na[:], 0.0, ALU.subtract, ALU.min).then_inc(z_done, 1)
            dve.wait_ge(score_done, 1)
            nc.vector.tensor_copy(work[:], score[:]).then_inc(work_done, 1)
            nc.vector.tensor_scalar(comp[:], score[:], -1.0, 1.0, ALU.mult, ALU.add).then_inc(comp_done, 1)
            dve.wait_ge(comp_done, 1)
            nc.vector.tensor_tensor(gate[:], score[:], comp[:], ALU.add).then_inc(gate_done, 1)
            for r in range(SLOTS // 8):
                dve.wait_ge(work_done, r + 1)
                nc.vector.max(top[:], work[:]).then_inc(top_done, 1)
                dve.wait_ge(top_done, r + 1)
                nc.vector.match_replace(work[:], top[:], work[:], -1.0).then_inc(work_done, 1)
            dve.wait_ge(work_done, SLOTS // 8 + 1)
            nc.vector.tensor_scalar(mask[:], work[:], 0.0, None, ALU.is_lt).then_inc(mask_done, 1)
            dve.wait_ge(turned, 1)
            nc.vector.tensor_copy(maskT[:], pt[:, 0].rearrange("p (t b) -> p t b", t=4)).then_inc(mT, 1)
            dve.wait_ge(c_ready, 6)
            nc.vector.tensor_copy(vals[:, :, :, 1], pt[:, 1].rearrange("p (t b) -> p t b", t=4)).then_inc(vT, 1)
            dve.wait_ge(mT, 1)
            dve.wait_ge(pos_done, 1)
            nc.vector.tensor_tensor(pm[:], pp[:], maskT[:], ALU.mult).then_inc(pm_done, 1)
            dve.wait_ge(pm_done, 1)
            nc.vector.tensor_scalar(slot[:], pm[:], -1.0, None, ALU.add).then_inc(slot_done, 1)
            dve.wait_ge(slot_done, 1)
            with dve.Fori(0, NB // 2) as m:
                for e in (0, 1):
                    b = m * 2 + e
                    dve.wait_ge(list_done, b + 1)
                    for t in range(4):
                        nc.vector.tensor_scalar(hot[:, e, t], slot_no[:], slot[:, t, bass.ds(b, 1)], None, ALU.is_equal).then_inc(hot_done, 1)
            dve.wait_ge(list_done, NB + 2)
            nc.vector.tensor_copy(idx[:], pl[:, :, :, 0].rearrange("p b h -> p (b h)")).then_inc(idx_done, 1)
            nc.vector.tensor_copy(gates[:], pl[:, :, :, 1].rearrange("p b h -> p (b h)")).then_inc(idx_done, 1)

        @block.scalar
        def _(act):
            with act.Fori(0, ITERS - 1) as k:
                act.wait_ge(sb_done, k + 1)
                act.wait_ge(nm_done, k + 1)
                nc.scalar.activation(ex[:], sb_[:], ACT.Exp, bias=nm[:], accum_out=tot[:]).then_inc(ex_done, 1)
                act.wait_ge(ex_done, k + 1)
                nc.scalar.activation(lg[:], tot[:], ACT.Ln).then_inc(ln_done, 1)
            act.wait_ge(z_done, 1)
            nc.scalar.activation(score[:], z[:], ACT.Exp).then_inc(score_done, 1)


def heavy_phase(nc, tag, xr_rows, x2, lidx, lgate, gamma, w1, b1, w2, b2):
    HID = 1024
    C, TILES = HID // P, 2 * NB // 4
    with ExitStack() as ctx:
        sb = lambda n, s, d=F32: ctx.enter_context(nc.sbuf_tensor(tag + n, s, d))
        ps = lambda n, s: ctx.enter_context(nc.psum_tensor(tag + n, s, F32))
        sem = phase_semaphores(nc, ctx, tag + "s_")
        ident = sb("ident", [P, P])
        w1_raw = sb("w1_raw", [P, 2, HID])
        w1g = sb("w1g", [P, 2, HID])
        gam = sb("gam", [P, 2])
        b1c = sb("b1c", [P, C])
        w2s = sb("w2s", [P, C, 256])
        b2r = sb("b2r", [P, 256])
        idx = sb("idx", [P, 2 * NB], I32)
        gates = sb("gates", [P, 2 * NB])
        cur = sb("cur", [P, 2, 4], I32)
        curg = sb("curg", [P, 2, 4])
        xg = sb("xg", [P, 2, 4, 256])
        xo = sb("xo", [P, 2, 4, 256])
        xgT = sb("xgT", [P, 2, 512])
        hid = sb("hid", [P, C, 512])
        yb = sb("yb", [P, 4, 256])
        res = sb("res", [P, 2, 4, 256])
        pa = ps("pa", [P, 2, 512])
        ph = ps("ph", [P, 2, 512])
        py = ps("py", [P, 4, 256])
        w_loaded, id0, id_ready, w1_ready = map(sem, ("w", "id0", "id1", "w1g"))
        cur_done, turned, xgT_done, h_done, gelu_done, y_done, yb_done, res_done = map(
            sem, ("cur", "turn", "xgT", "h", "gelu", "y", "yb", "res"))
        passed = sem("pass")
        fetched = [sem(f"f{e}") for e in (0, 1)]
        put = [sem(f"put{e}") for e in (0, 1)]
        block = ctx.enter_context(nc.Block())

        def tiles(eng, body):
            with eng.Fori(0, TILES // 2) as m:
                for e in (0, 1):
                    body(m * 2 + e, e, m)

        @block.sync
        def _(sp):
            with nc.allow_non_contiguous_dma(reason="small constants"):
                sp.dma_start(w1_raw[:], w1.rearrange("(k p) m -> p k m", p=P)).then_inc(w_loaded, 16)
                sp.dma_start(gam[:], gamma.rearrange("(k p) -> p k", p=P)).then_inc(w_loaded, 16)
                sp.dma_start(b1c[:], b1.rearrange("(c p) -> p c", p=P)).then_inc(w_loaded, 16)
                sp.dma_start(w2s[:], w2.rearrange("(c p) d -> p c d", p=P)).then_inc(w_loaded, 16)
                sp.dma_start(b2r[:], b2.partition_broadcast(P)).then_inc(w_loaded, 16)
                sp.dma_start(idx[:], lidx).then_inc(w_loaded, 16)
                sp.dma_start(gates[:], lgate).then_inc(w_loaded, 16)

        @block.gpsimd
        def _(pool):
            make_identity(nc, ident, id0, id_ready)

            def fetch(n, e):
                pool.wait_ge(cur_done, done(n, 2, 2))
                pool.wait_ge(turned, n + 1)
                pool.wait_ge(res_done, n * 4 + 4)
                pool.sem_inc(passed, 1)
                for dst, src in ((xg, xr_rows), (xo, x2)):
                    for j in range(4):
                        nc.gpsimd.indirect_dma_start(out=dst[:, e, j], out_offset=None, in_=src,
                                                     in_offset=bass.IndirectOffsetOnAxis(ap=cur[:, e, j:j + 1], axis=0)
                                                     ).then_inc(fetched[e], 16)

            def scatter(n, e):
                pool.wait_ge(res_done, n * 4 + 12)
                pool.sem_inc(passed, 1)
                for j in range(4):
                    nc.gpsimd.indirect_dma_start(out=x2, out_offset=bass.IndirectOffsetOnAxis(ap=cur[:, e, j:j + 1], axis=0),
                                                 in_=res[:, e, j], in_offset=None).then_inc(put[e], 16)

            fetch(0, 0)
            with pool.Fori(0, TILES // 2 - 1) as m:
                for e in (0, 1):
                    fetch(m * 2 + 1 + e, 1 - e)
                    scatter(m * 2 + e, e)
            fetch(TILES - 1, 1)
            scatter(TILES - 2, 0)
            scatter(TILES - 1, 1)
            for e in (0, 1):
                pool.wait_ge(put[e], 64 * TILES // 2)

        @block.tensor
        def _(pe):
            pe.wait_ge(id_ready, 1)
            pe.wait_ge(w1_ready, 2)
            credit(pe, [(turned, 2), (h_done, C), (y_done, 1)])

            def tile(n, e, m):
                pe.wait_ge(fetched[e], m * 128 + 128)
                pe.wait_ge(xgT_done, n + 1)
                for t in range(4):
                    for k in range(2):
                        mm = nc.tensor.transpose(pa[:, k, t * P:t * P + P], xg[:, e, t, k * P:k * P + P], ident[:])
                mm.then_inc(turned, 1)
                pe.wait_ge(xgT_done, n + 2)
                for c in range(C):
                    pe.wait_ge(gelu_done, n * C + C + c - 1)
                    for k in range(2):
                        mm = nc.tensor.matmul(ph[:, c % 2], w1g[:, k, c * P:c * P + P], xgT[:, k], start=(k == 0), stop=(k == 1))
                    mm.then_inc(h_done, 1)
                pe.wait_ge(yb_done, n + 1)
                for t in range(4):
                    for c in range(C):
                        if t == 0:
                            pe.wait_ge(gelu_done, n * C + C + c + 1)
                        mm = nc.tensor.matmul(py[:, t], hid[:, c, t * P:t * P + P], w2s[:, c], start=(c == 0), stop=(c == C - 1))
                mm.then_inc(y_done, 1)

            tiles(pe, tile)

        @block.vector
        def _(dve):
            dve.wait_ge(w_loaded, 16 * 7)
            for k in range(2):
                nc.vector.tensor_scalar(w1g[:, k], w1_raw[:, k], gam[:, k:k + 1], None, ALU.mult).then_inc(w1_ready, 1)
            credit(dve, [(cur_done, 2), (yb_done, 1), (res_done, 8)])

            def pick(n, e):
                nc.vector.tensor_copy(cur[:, e], idx[:, bass.ds(n * 4, 4)]).then_inc(cur_done, 1)
                nc.vector.tensor_copy(curg[:, e], gates[:, bass.ds(n * 4, 4)]).then_inc(cur_done, 1)

            def tile(n, e, m):
                dve.wait_ge(y_done, n + 2)
                dve.wait_ge(res_done, n * 4 + 8)
                nc.vector.tensor_tensor(yb[:], py[:], b2r[:].unsqueeze(1).to_broadcast([P, 4, 256]), ALU.add).then_inc(yb_done, 1)
                dve.wait_ge(yb_done, n + 2)
                for t in range(4):
                    nc.vector.scalar_tensor_tensor(res[:, e, t], yb[:, t], curg[:, e, t:t + 1], xo[:, e, t], ALU.mult, ALU.add
                                                   ).then_inc(res_done, 1)

            pick(0, 0)
            pick(1, 1)
            for e in (0, 1):
                tile(e, e, 0)
            with dve.Fori(1, TILES // 2) as m:
                for e in (0, 1):
                    dve.wait_ge(put[e], m * 64)
                    pick(m * 2 + e, e)
                    tile(m * 2 + e, e, m)

        @block.scalar
        def _(act):
            act.wait_ge(w_loaded, 16 * 7)
            credit(act, [(xgT_done, 1), (gelu_done, C)])

            def tile(n, e, m):
                act.wait_ge(turned, n + 3)
                act.wait_ge(h_done, n * C + C)
                nc.scalar.copy(xgT[:], pa[:]).then_inc(xgT_done, 1)
                for c in range(C):
                    act.wait_ge(h_done, n * C + C + c + 1)
                    if c == 0:
                        act.wait_ge(y_done, n + 1)
                    nc.scalar.activation(hid[:, c], ph[:, c % 2], ACT.Gelu, bias=b1c[:, c:c + 1]).then_inc(gelu_done, 1)

            tiles(act, tile)


HEADS, HD = 16, 16
HG = 4


def attention_phase(nc, tag, xin, Wq, Wk, Wv, xout):
    T, G, UN = 512, HEADS // HG, 16
    with ExitStack() as ctx:
        sb = lambda n, s, d=F32: ctx.enter_context(nc.sbuf_tensor(tag + n, s, d))
        ps = lambda n, s: ctx.enter_context(nc.psum_tensor(tag + n, s, F32))
        sem = phase_semaphores(nc, ctx, tag + "s_")
        ident = sb("ident", [P, P])
        w_raw = sb("w_raw", [P, 3, 2, 256])
        w_all = sb("w_all", [P, G, 3, 2, P])
        w_cur = sb("w_cur", [P, 3, 2, P])
        eps = sb("eps", [P, 1])
        xt = sb("xt", [P, 2, 4, 256])
        stats = sb("stats", [P, 4, 6])
        mv = sb("mv", [P, 4, 2])
        std = sb("std", [P, 4])
        rstd = sb("rstd", [P, 4])
        xl = sb("xl", [P, 4, 256])
        xlT = sb("xlT", [P, 2, T])
        qT = sb("qT", [P, T])
        kT = sb("kT", [P, T])
        v = sb("v", [P, 4, P])
        nmx = sb("nmx", [P, 4])
        al = sb("al", [P, 4, T])
        sums = sb("sums", [P, 4, HG])
        rec = sb("rec", [P, 4, HG])
        alT = sb("alT", [P, 2, 4, T])
        oT = sb("oT", [P, T])
        on = sb("on", [P, 4, HG, HD])
        pscore = ps("score", [P, 2, T])
        pt = ps("pt", [P, 2, 4, P])
        po = ps("po", [P, T])
        pq = ps("pq", [P, T])
        pk = ps("pk", [P, T])
        pv = ps("pv", [P, 4, P])
        id0, id_ready, eps_ready, w_loaded, w_zero, w_ready = map(sem, ("id0", "id1", "eps", "w", "wz", "wr"))
        x_loaded = [sem(f"x{e}") for e in (0, 1)]
        st_done, ag_done, std_done, rstd_done, xl_done, xl_turned, xlT_done, passed_d, passed_p = map(
            sem, ("st", "ag", "std", "rstd", "xl", "xlt", "xlT", "pd", "pp"))
        cur_done, q_done, k_done, v_done, q_put, k_put, v_put = map(sem, ("cur", "q", "k", "v", "qp", "kp", "vp"))
        s_done, mx_done, ex_done, mask_done, t_done, c_done, pv_done = map(sem, ("s", "mx", "ex", "mask", "t", "c", "pv"))
        o_put, o_turned, rec_done, norm_done, add_done, stored = map(sem, ("op", "ot", "rec", "norm", "add", "st2"))
        block = ctx.enter_context(nc.Block())

        def rows(eng, start, group):
            with eng.Fori(0, NB // 2) as m:
                for e in (0, 1):
                    start(m * 2 + e, e, m)
                    with eng.Fori(0, G) as g:
                        group((m * 2 + e) * G + g, g, e)

        @block.sync
        def _(sp):
            for x, w in enumerate((Wq, Wk, Wv)):
                sp.dma_start(w_raw[:, x], w.rearrange("(k p) m -> p k m", p=P)).then_inc(w_loaded, 16)
            credit(sp, [(stored, 32)])

            def load(n, e):
                sp.wait_ge(stored, n * 16 + 16)
                sp.dma_start(xt[:, e], xin[bass.ds(n * T, T), :].rearrange("(b p) d -> p b d", p=P)).then_inc(x_loaded[e], 16)

            def store(n, e):
                sp.wait_ge(add_done, n * G + G + 1)
                sp.dma_start(xout[bass.ds(n * T, T), :].rearrange("(b p) d -> p b d", p=P), xt[:, e]).then_inc(stored, 16)

            load(0, 0)
            with sp.Fori(0, NB // 2 - 1) as m:
                for e in (0, 1):
                    load(m * 2 + 1 + e, 1 - e)
                    store(m * 2 + e, e)
            load(NB - 1, 1)
            store(NB - 2, 0)
            store(NB - 1, 1)
            sp.wait_ge(stored, 16 * NB + 32)

        @block.gpsimd
        def _(pool):
            make_identity(nc, ident, id0, id_ready)
            nc.gpsimd.memset(w_all[:].rearrange("p g x k m -> p (g x k m)"), 0.0).then_inc(w_zero, 1)
            credit(pool, [(mask_done, UN)])

            def group(i, g, e):
                for u in range(UN):
                    qb = u % 4
                    pool.wait_ge(ex_done, i * UN + UN + u + 1)
                    pool.sem_inc(passed_p, 1)
                    d = al[:, u % 4, qb * P:qb * P + P]
                    nc.gpsimd.affine_select(out=d, in_=d, compare_op=ALU.is_ge, fill=0.0, base=0,
                                            pattern=[[-1, P]], channel_multiplier=1).then_inc(mask_done, 1)

            rows(pool, lambda n, e, m: None, group)

        @block.tensor
        def _(pe):
            pe.wait_ge(id_ready, 1)
            credit(pe, [(xl_turned, 1), (q_done, 1), (k_done, 1), (v_done, 1), (s_done, UN), (t_done, UN), (pv_done, 4), (o_turned, 1)])

            def start(n, e, m):
                pe.wait_ge(xl_done, n * 4 + 8)
                pe.wait_ge(k_put, n * G + 1)
                pe.wait_ge(q_put, n * G + 1)
                for t in range(4):
                    for k in range(2):
                        mm = nc.tensor.transpose((pq, pk)[k][:, t * P:t * P + P], xl[:, t, k * P:k * P + P], ident[:])
                mm.then_inc(xl_turned, 1)

            def scores(i, u):
                h, qb = divmod(u, 4)
                pe.wait_ge(ex_done, i * UN + UN + u - 1)
                nc.tensor.matmul(pscore[:, u % 2], qT[32 * h:32 * h + HD, qb * P:qb * P + P], kT[32 * h:32 * h + HD, :],
                                 start=True, stop=True).then_inc(s_done, 1)

            def turn(i, u):
                qb = u % 4
                pe.wait_ge(mask_done, i * UN + UN + u + 1)
                pe.wait_ge(c_done, i * UN + UN + u - 1)
                for kb in range(qb + 1):
                    mm = nc.tensor.transpose(pt[:, u % 2, kb], al[:, u % 4, kb * P:kb * P + P], ident[:])
                mm.then_inc(t_done, 1)

            def values(i, h):
                pe.wait_ge(c_done, i * UN + UN + 4 * h + 4)
                if h == 0:
                    pe.wait_ge(o_put, i + 1)
                    pe.wait_ge(v_put, i + 2)
                for kb in range(4):
                    mm = nc.tensor.matmul(po[32 * h:32 * h + 32, kb * P:], v[:, kb, 32 * h:32 * h + 32],
                                          alT[:, h % 2, kb, kb * P:], start=(kb == 0), stop=(kb == 3), skip_group_check=True)
                mm.then_inc(pv_done, 1)

            def group(i, g, e):
                pe.wait_ge(xlT_done, i // G + 2)
                pe.wait_ge(cur_done, i + 2)
                pe.wait_ge(q_put, i + 1)
                for k in range(2):
                    mm = nc.tensor.matmul(pq[:], w_cur[:, 0, k], xlT[:, k], start=(k == 0), stop=(k == 1))
                mm.then_inc(q_done, 1)
                pe.wait_ge(k_put, i + 1)
                for k in range(2):
                    mm = nc.tensor.matmul(pk[:], w_cur[:, 1, k], xlT[:, k], start=(k == 0), stop=(k == 1))
                mm.then_inc(k_done, 1)
                pe.wait_ge(norm_done, i + 1)
                for t in range(4):
                    for k in range(2):
                        mm = nc.tensor.matmul(pv[:, t], xlT[:, k, t * P:t * P + P], w_cur[:, 2, k], start=(k == 0), stop=(k == 1))
                mm.then_inc(v_done, 1)
                pe.wait_ge(q_put, i + 2)
                pe.wait_ge(k_put, i + 2)
                scores(i, 0)
                scores(i, 1)
                for u in range(UN):
                    if u + 2 < UN:
                        scores(i, u + 2)
                    turn(i, u)
                    if u % 4 == 1 and u > 4:
                        values(i, u // 4 - 1)
                values(i, 3)
                pe.wait_ge(o_put, i + 2)
                for t in range(4):
                    mm = nc.tensor.transpose(pv[:, t], oT[:, t * P:t * P + P], ident[:])
                mm.then_inc(o_turned, 1)

            rows(pe, start, group)

        @block.vector
        def _(dve):
            nc.vector.memset(eps[:], LN_EPS).then_inc(eps_ready, 1)
            dve.wait_ge(w_loaded, 48)
            dve.wait_ge(w_zero, 1)
            for g in range(G):
                for x in range(3):
                    for k in range(2):
                        src = w_raw[:, x, k, g * 64:g * 64 + 64].rearrange("p (h d) -> p h d", d=HD)
                        dst = w_all[:, g, x, k].rearrange("p (h d) -> p h d", d=32)[:, :, 0:HD]
                        nc.vector.tensor_scalar(dst, src, 0.25 if x == 0 else 1.0, None, ALU.mult).then_inc(w_ready, 1)
            dve.wait_ge(w_ready, 24)
            credit(dve, [(st_done, 4), (ag_done, 4), (rstd_done, 1), (xl_done, 4), (cur_done, 1), (v_put, 1), (mx_done, UN), (c_done, UN),
                         (rec_done, 1), (norm_done, 1), (add_done, 1)])

            def start(n, e, m):
                dve.wait_ge(x_loaded[e], m * 16 + 16)
                for t in range(4):
                    nc.vector.bn_stats(stats[:, t], xt[:, e, t]).then_inc(st_done, 1)
                for t in range(4):
                    dve.wait_ge(st_done, done(n, t + 1, 4))
                    dve.sem_inc(passed_d, 1)
                    nc.vector.bn_aggr(mv[:, t], stats[:, t]).then_inc(ag_done, 1)
                dve.wait_ge(std_done, done(n, 1))
                nc.vector.reciprocal(rstd[:], std[:]).then_inc(rstd_done, 1)
                dve.wait_ge(rstd_done, done(n, 1))
                dve.wait_ge(xl_turned, done(n, 0))
                for t in range(4):
                    nc.vector.tensor_scalar(xl[:, t], xt[:, e, t], mv[:, t, 0:1], rstd[:, t:t + 1], ALU.subtract, ALU.mult
                                            ).then_inc(xl_done, 1)

            def maximum(i, u):
                dve.wait_ge(s_done, i * UN + UN + u + 1)
                nc.vector.tensor_reduce(nmx[:, u % 4:u % 4 + 1], pscore[:, u % 2], AX_X, ALU.max, negate=True).then_inc(mx_done, 1)

            def copy(i, u):
                h, qb = divmod(u, 4)
                dve.wait_ge(t_done, i * UN + UN + u + 1)
                if qb == 0:
                    dve.wait_ge(pv_done, i * 4 + 4 + h - 1)
                nc.vector.tensor_copy(alT[:, h % 2, 0:qb + 1, qb * P:qb * P + P], pt[:, u % 2, 0:qb + 1]).then_inc(c_done, 1)

            def group(i, g, e):
                dve.wait_ge(v_done, i + 1)
                nc.vector.tensor_copy(w_cur[:], w_all[:, bass.ds(g, 1)].rearrange("p o x k m -> p (o x) k m")).then_inc(cur_done, 1)
                dve.wait_ge(v_done, i + 2)
                dve.wait_ge(pv_done, i * 4 + 4)
                nc.vector.tensor_copy(v[:], pv[:]).then_inc(v_put, 1)
                maximum(i, 0)
                maximum(i, 1)
                for u in range(UN):
                    if u + 2 < UN:
                        maximum(i, u + 2)
                    copy(i, u)
                dve.wait_ge(ex_done, i * UN + UN + UN)
                nc.vector.reciprocal(rec[:], sums[:]).then_inc(rec_done, 1)
                dve.wait_ge(rec_done, i + 2)
                dve.wait_ge(o_turned, i + 2)
                nc.vector.tensor_tensor(on[:], pv[:].rearrange("p t (h d) -> p t h d", h=HG)[:, :, :, 0:HD],
                                        rec[:].unsqueeze(3).to_broadcast([P, 4, HG, HD]), ALU.mult).then_inc(norm_done, 1)
                dve.wait_ge(norm_done, i + 2)
                cols = xt[:, e, :, bass.ds(g * 64, 64)]
                nc.vector.tensor_tensor(cols, cols, on[:].rearrange("p t h d -> p t (h d)"), ALU.add).then_inc(add_done, 1)

            rows(dve, start, group)

        @block.scalar
        def _(act):
            act.wait_ge(eps_ready, 1)
            credit(act, [(std_done, 1), (xlT_done, 1), (q_put, 1), (k_put, 1), (ex_done, UN), (o_put, 1)])

            def start(n, e, m):
                act.wait_ge(ag_done, done(n, 4, 4))
                act.wait_ge(rstd_done, done(n, 0))
                nc.scalar.activation(std[:], mv[:, :, 1], ACT.Sqrt, bias=eps[:]).then_inc(std_done, 1)
                act.wait_ge(xl_turned, done(n, 1))
                act.wait_ge(v_done, n * G + 1)
                nc.scalar.copy(xlT[:, 0], pq[:])
                nc.scalar.copy(xlT[:, 1], pk[:]).then_inc(xlT_done, 1)

            def group(i, g, e):
                act.wait_ge(q_done, i + 2)
                act.wait_ge(s_done, i * UN + UN)
                nc.scalar.copy(qT[:], pq[:]).then_inc(q_put, 1)
                act.wait_ge(k_done, i + 2)
                nc.scalar.copy(kT[:], pk[:]).then_inc(k_put, 1)
                act.wait_ge(rec_done, i + 1)
                for u in range(UN):
                    act.wait_ge(mx_done, i * UN + UN + u + 1)
                    act.wait_ge(t_done, i * UN + UN + u - 3)
                    h, qb = divmod(u, 4)
                    nc.scalar.activation(al[:, u % 4], pscore[:, u % 2], ACT.Exp, bias=nmx[:, u % 4:u % 4 + 1],
                                         accum_out=sums[:, qb, h:h + 1]).then_inc(ex_done, 1)
                act.wait_ge(pv_done, i * 4 + 8)
                act.wait_ge(o_turned, i + 1)
                nc.scalar.copy(oT[:], po[:]).then_inc(o_put, 1)

            rows(act, start, group)


def hybrid_block(nc, x, W_in, W_k, W_v, W_q, W_beta, b_beta, W_out, Wq, Wk, Wv, token, l_gamma, l_w1, l_b1, l_w2, l_b2,
                 h_gamma, h_w1, h_b1, h_w2, h_b2, out):
    T = x.shape[1]
    dram = lambda name, shape, dtype=F32: nc.dram_tensor(name, shape, dtype, kind="Internal").ap()
    kT = dram("kT_dram", (P, 64, T))
    qT = dram("qT_dram", (P, 64, T + 1))
    vbR = dram("vb_dram", (T, 12, 2, 2048), BF16)
    cell = dram("cell_dram", (T + U, 4, 4, 512))
    rows = dram("xr_dram", (NB * T, 256))
    scores = dram("s_dram", (NB, T))
    lidx = dram("idx_dram", (P, 2 * NB), I32)
    lgate = dram("gate_dram", (P, 2 * NB))
    x2 = dram("x2_dram", (NB * T, 256))
    x3 = dram("x3_dram", (NB, T, 256))
    flat = lambda a: a.rearrange("b t d -> (b t) d")

    project_phase(nc, x, W_in, W_k, W_v, W_q, W_beta, b_beta, kT, qT, vbR, T)
    scan_phase(nc, kT, qT, vbR, cell, T)
    light_phase(nc, "la", x, cell, W_out, l_gamma, l_w1, l_b1, l_w2, l_b2, token, x2, rows, scores)
    router_phase(nc, "ra", scores, lidx, lgate)
    heavy_phase(nc, "ha", rows, x2, lidx, lgate, h_gamma, h_w1, h_b1, h_w2, h_b2)
    attention_phase(nc, "at", x2, Wq, Wk, Wv, flat(x3))
    light_phase(nc, "lb", x3, None, None, l_gamma, l_w1, l_b1, l_w2, l_b2, token, flat(out), rows, scores)
    router_phase(nc, "rb", scores, lidx, lgate)
    heavy_phase(nc, "hb", rows, flat(out), lidx, lgate, h_gamma, h_w1, h_b1, h_w2, h_b2)


_INS = ['L0_attn_a_x', 'L0_attn_a_W_in', 'L0_attn_a_W_k', 'L0_attn_a_W_v', 'L0_attn_a_W_q', 'L0_attn_a_W_beta',
        'L0_attn_a_b_beta', 'L0_attn_a_W_out', 'L0_attn_b_Wq', 'L0_attn_b_Wk', 'L0_attn_b_Wv', 'L0_ffn_routing_token',
        'L0_ffn_light_gamma', 'L0_ffn_light_w1', 'L0_ffn_light_b1', 'L0_ffn_light_w2', 'L0_ffn_light_b2',
        'L0_ffn_heavy_gamma', 'L0_ffn_heavy_w1', 'L0_ffn_heavy_b1', 'L0_ffn_heavy_w2', 'L0_ffn_heavy_b2']
_OUTS = [((32, 512, 256), 'float32')]


def kernel(**inputs):
    import numpy as _np
    import concourse.bacc as _bacc
    from concourse import mybir as _mybir
    from concourse.bass_utils import run_bass_kernel_spmd as _run

    nc = _bacc.Bacc("TRN2", target_bir_lowering=False, num_devices=1)
    arrays, args = {}, []
    for name in _INS:
        a = _np.ascontiguousarray(inputs[name])
        arrays[f"in_{name}_dram"] = a
        args.append(nc.dram_tensor(f"in_{name}_dram", a.shape, _mybir.dt.from_np(a.dtype), kind="ExternalInput").ap())
    for i, (shape, dtype) in enumerate(_OUTS):
        dt = _mybir.dt.from_np(_np.dtype(dtype))
        args.append(nc.dram_tensor(f"out_{i}_dram", shape, dt, kind="ExternalOutput").ap())
    hybrid_block(nc, *args)
    r = _run(nc, [arrays], core_ids=[0])
    return r.results[0]["out_0_dram"]
```

```python
import math
from contextlib import ExitStack
import concourse.bass as bass
from concourse import mybir

F32 = mybir.dt.float32
BF16 = mybir.dt.bfloat16
ALU = mybir.AluOpType
ACT = mybir.ActivationFunctionType
AX_X = mybir.AxisListType.X
P = 128
NB = 32
NH = 8
N = 32
TB = 32
U = 8


def phase_semaphores(nc, ctx, prefix):
    own = []

    def clear():
        nc.all_engine_barrier()
        nc.clear_and_free_semaphores(own)
        nc.all_engine_barrier()

    def sem(name):
        own.append(nc.alloc_semaphore(name=prefix + name))
        return own[-1]

    ctx.callback(clear)
    return sem


def make_identity(nc, ident, made, ready):
    nc.gpsimd.memset(ident[:], 0.0).then_inc(made, 1)
    nc.gpsimd.wait_ge(made, 1)
    nc.gpsimd.affine_select(out=ident[:], in_=ident[:], compare_op=ALU.not_equal, fill=1.0, base=0,
                            pattern=[[-1, P]], channel_multiplier=1).then_inc(ready, 1)


def scan_phase(nc, kT, qT, vbR, cell, T):
    CH, SETS = T // TB, T // U
    with ExitStack() as ctx:
        sb = lambda n, s, d=F32: ctx.enter_context(nc.sbuf_tensor(n, s, d))
        ps = lambda n, s: ctx.enter_context(nc.psum_tensor(n, s, F32))
        sem = phase_semaphores(nc, ctx, "c")
        state = sb("state", [P, 2, 2, 1024])
        scaled = sb("scaled", [P, 2, 1024])
        kprod = sb("kprod", [P, 2, 1024])
        qprod = sb("qprod", [P, 2, 1024])
        blocks = sb("blocks", [P, P])
        spread = sb("spread", [12, P], BF16)
        pick = sb("pick", [P, U, 32])
        kbuf = sb("kbuf", [P, 2, 64, TB])
        qbuf = sb("qbuf", [P, 2, 64, TB])
        qlast = sb("qlast", [P, 64, 1])
        rows = sb("rows", [12, 2, 4, 2, 2048], BF16)
        outs = sb("outs", [P, 512])
        diff = ps("diff", [P, 2, 1024])
        beta = ps("beta", [P, 1024])
        sums = ps("sums", [P, 512])

        ones_made, blocks_made, spread_made, pick_made, pick_ready = map(
            sem, ("s_ones", "s_blocks", "s_spread", "s_pick", "s_pickr"))
        state_ready = [sem(f"s_state{u}") for u in (0, 1)]
        kprod_ready = [sem(f"s_kp{u}") for u in (0, 1)]
        qprod_ready = [sem(f"s_qp{u}") for u in (0, 1)]
        diff_ready = [sem(f"s_diff{u}") for u in (0, 1)]
        beta_ready, scaled_ready = sem("s_beta"), sem("s_scaled")
        outer_ready = [sem(f"s_outer{u}") for u in (0, 1)]
        sum_ready = [sem(f"s_sum{u}") for u in (0, 1)]
        qsum_done = [sem(f"s_qsum{u}") for u in (0, 1)]
        outs_copied = sem("s_outs")
        sp_passed = sem("s_sppass")
        stored, last_loaded = sem("s_stored"), sem("s_qlast")
        loaded = [sem(f"s_load{r}") for r in (0, 1)]
        rows_loaded = [sem(f"s_rows{r}") for r in (0, 1)]
        LOADS = 16 * 2

        def steps(eng, body, chunk_start=None):
            with eng.Fori(0, CH // 2) as pair:
                for r in (0, 1):
                    with eng.Fori(0, TB // U) as k:
                        n = (pair * 2 + r) * (TB // U) + k
                        for e in range(U):
                            if e == 0 and chunk_start:
                                chunk_start(pair, r)
                            body(n * U + e, r, k * U + e, e, n)

        block = ctx.enter_context(nc.Block())

        @block.sync
        def _(sp):
            def load(c, r):
                now = bass.ds(c * TB, TB)
                sp.dma_start(kbuf[:, r], kT[:, :, now]).then_inc(loaded[r], 16)
                sp.dma_start(qbuf[:, r], qT[:, :, now]).then_inc(loaded[r], 16)

            def load_rows(m, r):
                sp.dma_start(rows[:, r], vbR[bass.ds(m * 4, 4)].rearrange("t k x c -> k t (x c)")
                             ).then_inc(rows_loaded[r], 16)

            def sets(n0, n1, ahead=True):
                with sp.Fori(n0, n1) as n:
                    for r in (0, 1):
                        sp.wait_ge(diff_ready[1], n * U + 4 * r + 4)
                        if ahead:
                            load_rows(n * 2 + 2 + r, r)

            load_rows(0, 0)
            load_rows(1, 1)
            load(0, 0)
            load(1, 1)
            with nc.allow_non_contiguous_dma(reason="one column"):
                sp.dma_start(qlast[:], qT[:, :, T:T + 1]).then_inc(last_loaded, 16)
            K = TB // U
            with sp.Fori(0, CH // 2 - 1) as pair:
                for r in (0, 1):
                    sets((pair * 2 + r) * K, (pair * 2 + r) * K + K)
                    sp.wait_ge(sum_ready[1], (pair * 2 + r) * TB + TB + 1)
                    sp.sem_inc(sp_passed, 1)
                    sp.wait_ge(qprod_ready[1], (pair * 2 + r) * TB + TB + 1)
                    load(pair * 2 + r + 2, r)
            sets((CH - 2) * K, SETS - 1)

        @block.gpsimd
        def _(pool):
            nc.gpsimd.memset(blocks[:], -1.0).then_inc(ones_made, 1)
            pool.wait_ge(ones_made, 1)
            v = blocks[:].rearrange("p (q j) -> p q j", q=4)
            nc.gpsimd.affine_select(out=v, in_=v, compare_op=ALU.is_ge, fill=0.0, base=0,
                                    pattern=[[-32, 4], [0, 32]], channel_multiplier=1).then_inc(ones_made, 1)
            pool.wait_ge(ones_made, 2)
            nc.gpsimd.affine_select(out=v, in_=v, compare_op=ALU.is_ge, fill=0.0, base=31,
                                    pattern=[[32, 4], [0, 32]], channel_multiplier=-1).then_inc(blocks_made, 1)
            nc.gpsimd.memset(spread[:], 0.0).then_inc(spread_made, 1)
            for s in range(3):
                pool.wait_ge(spread_made, s + 1)
                v = spread[:].rearrange("k (q j) -> k q j", q=4)
                nc.gpsimd.affine_select(out=v, in_=v, compare_op=ALU.not_equal, fill=1.0, base=-4 * s,
                                        pattern=[[-1, 4], [0, 32]], channel_multiplier=1).then_inc(spread_made, 1)
            nc.gpsimd.memset(pick[:].rearrange("p e m -> p (e m)"), 0.0).then_inc(pick_made, 1)
            pool.wait_ge(blocks_made, 1)
            pool.wait_ge(pick_made, 1)
            for e in range(U):
                nc.gpsimd.tensor_scalar(pick[:, e, 4 * e:4 * e + 4], blocks[:, 0:P:32], -1.0, None, ALU.mult
                                        ).then_inc(pick_ready, 1)

            def arrived(pair, r):
                pool.wait_ge(loaded[r], pair * LOADS + LOADS)

            heads = lambda x, m: x[:, 0:N * m].rearrange("p (c i) -> p c i", i=N)
            for u in (0, 1):
                nc.gpsimd.memset(qprod[:, u], 0.0).then_inc(qprod_ready[u], 1)

            def step(t, r, tt, e, n):
                S = state[:, e % 2]
                for u in (0, 1):
                    pool.wait_ge(state_ready[u], t + 1)
                    for w in (0, 1):
                        c = slice(512 * w, 512 * w + 512)
                        nc.gpsimd.tensor_tensor(heads(kprod[:, u, c], 16), heads(S[:, u, c], 16),
                                                kbuf[:, r, 32 * u + 16 * w:32 * u + 16 * w + 16, bass.ds(tt, 1)].to_broadcast([P, 16, N]),
                                                ALU.mult).then_inc(kprod_ready[u], 1)
                    pool.wait_ge(qsum_done[u], t + 1 + u)
                    nc.gpsimd.tensor_tensor(heads(qprod[:, u], 32), heads(S[:, u], 32),
                                            qbuf[:, r, 32 * u:32 * u + 32, bass.ds(tt, 1)].to_broadcast([P, 32, N]),
                                            ALU.mult).then_inc(qprod_ready[u], 1)

            steps(pool, step, arrived)
            pool.wait_ge(last_loaded, 16)
            for u in (0, 1):
                pool.wait_ge(state_ready[u], T + 1)
                pool.wait_ge(qsum_done[u], T + 1 + u)
                nc.gpsimd.tensor_tensor(heads(qprod[:, u], 32), heads(state[:, 0, u], 32),
                                        qlast[:, 32 * u:32 * u + 32].to_broadcast([P, 32, N]), ALU.mult
                                        ).then_inc(qprod_ready[u], 1)

        @block.tensor
        def _(pe):
            pe.wait_ge(blocks_made, 1)
            pe.wait_ge(spread_made, 4)
            pe.wait_ge(pick_ready, U)

            def step(t, r, tt, e, n):
                if e % 4 == 0:
                    pe.wait_ge(rows_loaded[e // 4], n * 16 + 16)
                def spread_beta(u):
                    pe.wait_ge(scaled_ready, t * 2 + u + 1)
                    for w in (0, 1):
                        c = 1024 * u + 512 * w
                        mm = nc.tensor.matmul(beta[:, 512 * w:512 * w + 512], spread[:],
                                              rows[:, e // 4, e % 4, 1, c:c + 512], start=True, stop=True)
                    mm.then_inc(beta_ready, 1)

                def spread_v(u):
                    pe.wait_ge(state_ready[u], t + 1)
                    for w in (0, 1):
                        c = 1024 * u + 512 * w
                        nc.tensor.matmul(diff[:, u, 512 * w:512 * w + 512], spread[:],
                                         rows[:, e // 4, e % 4, 0, c:c + 512], start=True, stop=False)

                def retrieve(u):
                    for w in (0, 1):
                        pe.wait_ge(kprod_ready[u], t * 2 + w + 1)
                        mm = nc.tensor.matmul(diff[:, u, 512 * w:512 * w + 512], blocks[:],
                                              kprod[:, u, 512 * w:512 * w + 512], start=False, stop=True)
                    mm.then_inc(diff_ready[u], 1)

                spread_beta(0)
                spread_v(0)
                sums_of(1, t - 1, (e - 1) % U)
                retrieve(0)
                spread_beta(1)
                spread_v(1)
                if e == 0:
                    pe.wait_ge(outs_copied, n + 1)
                sums_of(0, t, e)
                retrieve(1)

            def sums_of(u, t, e, start=False):
                pe.wait_ge(qprod_ready[u], t + 2)
                for w in (0, 1):
                    z = 2 * u + w
                    mm = nc.tensor.matmul(sums[32 * z:32 * z + 32, :], pick[:, e], qprod[:, u, 512 * w:512 * w + 512],
                                          start=start or (e == 0), stop=(e == U - 1), skip_group_check=True)
                mm.then_inc(qsum_done[u], 1)

            for u in (0, 1):
                sums_of(u, -1, U - 1, start=True)
            steps(pe, step)
            sums_of(1, T - 1, U - 1)
            pe.wait_ge(outs_copied, SETS + 1)
            for u in (0, 1):
                sums_of(u, T, 0)

        @block.vector
        def _(dve):
            for u in (0, 1):
                nc.vector.memset(state[:, 0, u], 0.0).then_inc(state_ready[u], 1)
                dve.sem_inc(sum_ready[u], 1)
            dve.sem_inc(scaled_ready, 1)

            def arrived(pair, r):
                dve.wait_ge(loaded[r], pair * LOADS + LOADS)

            def step(t, r, tt, e, n):
                S = state[:, e % 2]
                for u in (0, 1):
                    dve.wait_ge(state_ready[u], t + 1)
                    dve.wait_ge(beta_ready, t * 2 + u + 1)
                    nc.vector.tensor_tensor(scaled[:, u], beta[:], S[:, u], ALU.mult).then_inc(scaled_ready, 1)
                    dve.wait_ge(diff_ready[u], t + 1)
                    o = diff[:, u].rearrange("p (c i) -> p c i", i=N)
                    nc.vector.tensor_tensor(o, o, kbuf[:, r, 32 * u:32 * u + 32, bass.ds(tt, 1)].to_broadcast([P, 32, N]),
                                            ALU.mult).then_inc(outer_ready[u], 1)
                    dve.wait_ge(outer_ready[u], t + 1)
                    dve.wait_ge(scaled_ready, t * 2 + u + 2)
                    nc.vector.tensor_tensor(diff[:, u], diff[:, u], scaled[:, u], ALU.add).then_inc(sum_ready[u], 1)

            steps(dve, step, arrived)

        @block.scalar
        def _(act):
            act.sem_inc(stored, 64)

            def put_out(n, t):
                act.wait_ge(qsum_done[1], t + 2)
                act.wait_ge(stored, n * 64 + 64)
                nc.scalar.copy(outs[:], sums[:]).then_inc(outs_copied, 1)
                act.wait_ge(outs_copied, n + 1)
                for z in range(4):
                    act.dma_start(cell[bass.ds(n * U, U), z], outs[32 * z:32 * z + 32]).then_inc(stored, 16)

            def step(t, r, tt, e, n):
                if e == 0:
                    put_out(n, t)
                for u in (0, 1):
                    act.wait_ge(sum_ready[u], t + 2)
                    act.wait_ge(qprod_ready[u], t + 1)
                    nc.scalar.activation(state[:, (e + 1) % 2, u], diff[:, u], ACT.Tanh).then_inc(state_ready[u], 1)

            steps(act, step)
            put_out(SETS, T)
            act.wait_ge(qsum_done[0], T + 2)
            put_out(SETS + 1, T + 1)
            act.wait_ge(stored, (SETS + 2) * 64 + 64)


def done(n, k=1, per=1):
    return n * per + k + per


def credit(eng, sems):
    for s, per in sems:
        eng.sem_inc(s, per)


def turn_weights(nc, block, jobs, stage, ps, ident, ident_ready, sem):
    w_loaded = [sem(f"s_wload{e}") for e in (0, 1)]
    w_turned, w_put = sem("s_wturn"), sem("s_wput")
    J = len(jobs)

    def loads(sp):
        for j, (w, _) in enumerate(jobs):
            if j >= 2:
                sp.wait_ge(w_turned, j - 1)
            R = w.shape[0] // P
            sp.dma_start(stage[:, j % 2, 0:R], w.rearrange("(r p) e -> p r e", p=P)).then_inc(w_loaded[j % 2], 16)

    def turns(pe):
        pe.wait_ge(ident_ready, 1)
        for j, (w, _) in enumerate(jobs):
            R = w.shape[0] // P
            pe.wait_ge(w_loaded[j % 2], 16 * (j // 2 + 1))
            if j >= 2:
                pe.wait_ge(w_put, j - 1)
            for r in range(R):
                for k in range(2):
                    mm = nc.tensor.transpose(ps[:, j % 2, (2 * r + k) * P:(2 * r + k + 1) * P], stage[:, j % 2, r, k * P:k * P + P], ident[:])
            mm.then_inc(w_turned, 1)

    def puts(dve):
        for j, (w, target) in enumerate(jobs):
            R = w.shape[0] // P
            dve.wait_ge(w_turned, j + 1)
            for r in range(R):
                for k in range(2):
                    src = ps[:, j % 2, (2 * r + k) * P:(2 * r + k + 1) * P]
                    dst = target(k, r)
                    if len(dst.shape) == 3:
                        src = src.rearrange("p (q i) -> p q i", q=4)
                    last = nc.vector.tensor_copy(dst, src)
            last.then_inc(w_put, 1)

    return loads, turns, puts, w_put


def project_phase(nc, x, W_in, W_k, W_v, W_q, W_beta, b_beta, kT, qT, vbR, T):
    TT = T // P
    EPS = 1e-5
    with ExitStack() as ctx:
        sb = lambda n, s, d=F32: ctx.enter_context(nc.sbuf_tensor(n, s, d))
        ps = lambda n, s: ctx.enter_context(nc.psum_tensor(n, s, F32))
        sem = phase_semaphores(nc, ctx, "p")
        ident = sb("p_ident", [P, P])
        w_stage = sb("w_stage", [P, 2, 2, 256])
        w_in = sb("w_in", [P, 2, 256])
        w_k = sb("w_k", [P, 2, 256])
        w_q = sb("w_q", [P, 2, 256])
        w_vb = sb("w_vb", [P, 2, 2, 4, 2, 32])
        bias = sb("bias", [P, 4, 2, 32])
        eps = sb("eps", [P, 1])
        xt = sb("xt", [P, 2, 4, 256])
        stats = sb("stats", [P, 4, 6])
        mv = sb("mv", [P, 4, 2])
        std = sb("std", [P, 4])
        rstd = sb("rstd", [P, 4])
        xn = sb("xn", [P, 4, 256])
        xnT = sb("xnT", [P, 2, 512])
        sig = sb("sig", [P, 2, 512])
        xp = sb("xp", [P, 2, 512])
        ksq = sb("ksq", [P, 4, 256])
        ksum = sb("ksum", [P, 32])
        knorm = sb("knorm", [P, 32])
        kinv = sb("kinv", [P, 32])
        kn = sb("kn", [P, 4, 256])
        k_out = sb("k_out", [P, 8, P])
        q_out = sb("q_out", [P, 8, P])
        vb = sb("vb", [P, 4, 2, 4, 64])
        parts = sb("parts", [P, 3, 2048], BF16)
        rest = sb("rest", [P, 2, 2048])
        zero = sb("zero", [P, 64, 1])
        turned = ps("p_turned", [P, 2, 512])
        xpp = ps("p_xp", [P, 2, 512])
        kk = ps("p_k", [P, 4, 256])
        vbp = ps("p_vb", [P, 2, 512])

        ident_zero, ident_ready, eps_ready, zero_ready, zero_stored, bias_loaded = map(
            sem, ("s_id0", "s_id1", "s_eps", "s_zero", "s_zst", "s_bias"))
        x_loaded = [sem(f"s_x{e}") for e in (0, 1)]
        stats_done, aggr_done, std_done, rstd_done, xn_done, x_turned, xnT_done, xpp_done = map(
            sem, ("s_st", "s_ag", "s_std", "s_rstd", "s_xn", "s_xt", "s_xnT", "s_xpp"))
        sig_done, xp_done, k_done, q_done, ksq_done, ksum_done, knorm_done, keps_done, kinv_done, kn_done, k_turned = map(
            sem, ("s_sig", "s_xp", "s_k", "s_q", "s_ksq", "s_ksum", "s_knorm", "s_keps", "s_kinv", "s_kn", "s_kt"))
        k_put, q_put, vb_done, v_put, b_put, b_sig = map(sem, ("s_kput", "s_qput", "s_vb", "s_vput", "s_bput", "s_bsig"))
        part1, rest1, part2, part3 = map(sem, ("s_part1", "s_rest1", "s_part2", "s_part3"))
        dve_passed = sem("s_dpass")
        k_stored, q_stored, vb_stored = map(sem, ("s_kst", "s_qst", "s_vbst"))

        jobs = [(W_in, lambda k, r: w_in[:, k, r * P:r * P + P]),
                (W_k, lambda k, r: w_k[:, k, r * P:r * P + P]),
                (W_q, lambda k, r: w_q[:, k, r * P:r * P + P]),
                (W_v, lambda k, r: w_vb[:, k, 0, :, r, :]),
                (W_beta, lambda k, r: w_vb[:, k, 1, :, r, :])]
        block = ctx.enter_context(nc.Block())
        loads, turns, puts, w_put = turn_weights(nc, block, jobs, w_stage, turned, ident, ident_ready, sem)

        TILES = NB // 4 * TT

        def tiles(eng, starts, body):
            for start in starts:
                start(0, 0)
            with eng.Fori(0, TILES // 2 - 1) as m:
                for e in (0, 1):
                    body(m * 2 + e, e, lambda k: starts[k](m * 2 + e + 1, 1 - e))
            body(TILES - 2, 0, lambda k: starts[k](TILES - 1, 1))
            body(TILES - 1, 1, lambda k: None)

        @block.sync
        def _(sp):
            loads(sp)
            with nc.allow_non_contiguous_dma(reason="rows of 128 bytes"):
                for f in range(2):
                    src = b_beta.rearrange("(f q) i -> f q i", f=2)[f]
                    sp.dma_start(bias[:, :, f], src.partition_broadcast(P)).then_inc(bias_loaded, 16)
            sp.wait_ge(zero_ready, 1)
            with nc.allow_non_contiguous_dma(reason="one column"):
                sp.dma_start(qT[:, :, 0:1], zero[:]).then_inc(zero_stored, 16)

            def load(n, e):
                sp.wait_ge(xn_done, done(n, 0, 4))
                sp.dma_start(xt[:, e], x[bass.ds(n // TT * 4, 4), bass.ds(n % TT * P, P), :].rearrange("b t d -> t b d")
                             ).then_inc(x_loaded[e], 16)

            def store(n):
                B, tt = n // TT, n % TT
                sp.wait_ge(q_put, done(n, 1))
                sp.dma_start(qT[:, bass.ds(B * 8, 8), bass.ds(tt * P + 1, P)], q_out[:]).then_inc(q_stored, 16)
                sp.wait_ge(k_put, done(n, 1))
                sp.dma_start(kT[:, bass.ds(B * 8, 8), bass.ds(tt * P, P)], k_out[:]).then_inc(k_stored, 16)
                sp.wait_ge(part3, done(n, 1))
                sp.dma_start(vbR[bass.ds(tt * P, P), :, :, bass.ds(B * 256, 256)].rearrange("t k x c -> t (k x) c"),
                             parts[:].rearrange("p s (m c) -> p (s m) c", c=256)).then_inc(vb_stored, 16)

            credit(sp, [(k_stored, 16), (q_stored, 16), (vb_stored, 16)])
            load(0, 0)
            load(1, 1)
            with sp.Fori(0, TILES // 2 - 1) as m:
                for e in (0, 1):
                    load(m * 2 + 2 + e, e)
                    store(m * 2 + e)
            store(TILES - 2)
            store(TILES - 1)
            for s in (k_stored, q_stored, vb_stored):
                sp.wait_ge(s, 16 * (TILES + 1))
            sp.wait_ge(zero_stored, 16)

        @block.gpsimd
        def _(pool):
            make_identity(nc, ident, ident_zero, ident_ready)
            nc.gpsimd.memset(zero[:], 0.0).then_inc(zero_ready, 1)

        @block.tensor
        def _(pe):
            turns(pe)
            pe.wait_ge(w_put, len(jobs))
            credit(pe, [(x_turned, 1), (xpp_done, 1), (k_done, 1), (q_done, 1), (vb_done, 2), (k_turned, 1)])

            def turn_x(n, e):
                pe.wait_ge(xn_done, done(n, 4, 4) + 4)
                pe.wait_ge(q_put, done(n, 0))
                for b in range(4):
                    for k in range(2):
                        mm = nc.tensor.transpose(turned[:, k, b * P:b * P + P], xn[:, b, k * P:k * P + P], ident[:])
                mm.then_inc(x_turned, 1)

            def tile(n, e, ahead):
                pe.wait_ge(xnT_done, done(n, 1))
                pe.wait_ge(k_put, done(n, 0))
                for c in range(2):
                    for k in range(2):
                        mm = nc.tensor.matmul(xpp[:, c], w_in[:, k, c * P:c * P + P], xnT[:, k], start=(k == 0), stop=(k == 1))
                mm.then_inc(xpp_done, 1)
                pe.wait_ge(xp_done, done(n, 1))
                pe.wait_ge(kn_done, done(n, 0))
                for b in range(4):
                    for k in range(2):
                        mm = nc.tensor.matmul(kk[:, b], xp[:, k, b * P:b * P + P], w_k[:, k], start=(k == 0), stop=(k == 1))
                mm.then_inc(k_done, 1)
                for h in range(2):
                    pe.wait_ge(v_put, done(n, 2 * h, 4))
                    pe.wait_ge(b_put, done(n, 2 * h, 4))
                    for b in (2 * h, 2 * h + 1):
                        for k in range(2):
                            mm = nc.tensor.matmul(vbp[:, b % 2], xp[:, k, b * P:b * P + P],
                                                  w_vb[:, k].rearrange("p x q f i -> p (x q f i)"), start=(k == 0), stop=(k == 1))
                    mm.then_inc(vb_done, 1)
                    if h == 0:
                        for f in range(2):
                            for k in range(2):
                                mm = nc.tensor.matmul(turned[:, f], w_q[:, k, f * P:f * P + P], xp[:, k], start=(k == 0), stop=(k == 1))
                        mm.then_inc(q_done, 1)
                pe.wait_ge(kn_done, done(n, 1))
                for b in range(4):
                    for f in range(2):
                        mm = nc.tensor.transpose(xpp[:, f, b * P:b * P + P], kn[:, b, f * P:f * P + P], ident[:])
                mm.then_inc(k_turned, 1)
                ahead(0)

            tiles(pe, [turn_x], tile)

        @block.vector
        def _(dve):
            nc.vector.memset(eps[:], EPS).then_inc(eps_ready, 1)
            puts(dve)
            credit(dve, [(stats_done, 4), (aggr_done, 4), (rstd_done, 1), (xn_done, 8), (xnT_done, 1), (xp_done, 1), (ksum_done, 1),
                         (keps_done, 1), (kinv_done, 1), (kn_done, 1), (k_put, 1), (b_put, 4), (rest1, 1), (part3, 1)])
            dve.wait_ge(bias_loaded, 32)

            def normalise(n, e):
                dve.wait_ge(x_loaded[e], (n - e) * 8 + 16)
                for b in range(4):
                    nc.vector.bn_stats(stats[:, b], xt[:, e, b]).then_inc(stats_done, 1)
                for b in range(4):
                    dve.wait_ge(stats_done, done(n, b + 1, 4))
                    dve.sem_inc(dve_passed, 1)
                    nc.vector.bn_aggr(mv[:, b], stats[:, b]).then_inc(aggr_done, 1)
                dve.wait_ge(std_done, done(n, 1))
                nc.vector.reciprocal(rstd[:], std[:]).then_inc(rstd_done, 1)
                dve.wait_ge(rstd_done, done(n, 1))
                dve.wait_ge(x_turned, done(n, 0))
                for b in range(4):
                    nc.vector.tensor_scalar(xn[:, b], xt[:, e, b], mv[:, b, 0:1], rstd[:, b:b + 1], ALU.subtract, ALU.mult
                                            ).then_inc(xn_done, 1)

            def put_x(n, e):
                dve.wait_ge(x_turned, done(n, 1))
                nc.vector.tensor_copy(xnT[:], turned[:]).then_inc(xnT_done, 1)

            def silu(n, e):
                dve.wait_ge(sig_done, done(n, 1))
                nc.vector.tensor_tensor(xp[:], xpp[:], sig[:], ALU.mult).then_inc(xp_done, 1)

            def tile(n, e, ahead):
                ahead(0)
                dve.wait_ge(ksq_done, done(n, 1))
                nc.vector.tensor_reduce(ksum[:], ksq[:].rearrange("p b (h j) -> p (b h) j", j=N), AX_X, ALU.add).then_inc(ksum_done, 1)
                dve.wait_ge(knorm_done, done(n, 1))
                nc.vector.tensor_scalar(knorm[:], knorm[:], 1e-6, None, ALU.add).then_inc(keps_done, 1)
                dve.wait_ge(keps_done, done(n, 1))
                nc.vector.reciprocal(kinv[:], knorm[:]).then_inc(kinv_done, 1)
                dve.wait_ge(kinv_done, done(n, 1))
                nc.vector.tensor_tensor(kn[:].rearrange("p b (h j) -> p (b h) j", j=N), kk[:].rearrange("p b (h j) -> p (b h) j", j=N),
                                        kinv[:].unsqueeze(2).to_broadcast([P, 32, N]), ALU.mult).then_inc(kn_done, 1)
                for b in range(4):
                    dve.wait_ge(vb_done, done(n, b // 2 + 1, 2))
                    if b == 0:
                        dve.wait_ge(part1, done(n, 0))
                    nc.vector.tensor_tensor(vb[:, :, 1, b], vbp[:, b % 2, 256:512].rearrange("p (q c) -> p q c", q=4),
                                            bias[:].rearrange("p q f i -> p q (f i)"), ALU.add).then_inc(b_put, 1)
                dve.wait_ge(k_turned, done(n, 1))
                dve.wait_ge(k_stored, done(n, 0, 16))
                nc.vector.tensor_copy(k_out[:].rearrange("p (b f) t -> p f b t", f=2),
                                      xpp[:].rearrange("p f (b t) -> p f b t", b=4)).then_inc(k_put, 1)
                ahead(1)
                dve.wait_ge(part1, done(n, 1))
                flat = vb[:].rearrange("p q x b c -> p (q x b c)")
                nc.vector.tensor_tensor(rest[:, 0], flat, parts[:, 0], ALU.subtract).then_inc(rest1, 1)
                ahead(2)
                dve.wait_ge(part2, done(n, 1))
                nc.vector.tensor_tensor(parts[:, 2], rest[:, 0], parts[:, 1], ALU.subtract).then_inc(part3, 1)

            tiles(dve, [normalise, put_x, silu], tile)

        @block.scalar
        def _(act):
            credit(act, [(part1, 1), (part2, 1), (std_done, 1), (sig_done, 1), (ksq_done, 1), (knorm_done, 1), (q_put, 1), (v_put, 4), (b_sig, 1)])
            act.wait_ge(eps_ready, 1)

            def deviations(n, e):
                act.wait_ge(aggr_done, done(n, 4, 4))
                act.wait_ge(rstd_done, done(n, 0))
                nc.scalar.activation(std[:], mv[:, :, 1], ACT.Sqrt, bias=eps[:]).then_inc(std_done, 1)

            def sigmoid(n, e):
                act.wait_ge(xpp_done, done(n, 1))
                act.wait_ge(xp_done, done(n, 0))
                nc.scalar.activation(sig[:], xpp[:], ACT.Sigmoid).then_inc(sig_done, 1)

            def tile(n, e, ahead):
                ahead(0)
                act.wait_ge(k_done, done(n, 1))
                act.wait_ge(ksum_done, done(n, 0))
                nc.scalar.activation(ksq[:], kk[:], ACT.Square).then_inc(ksq_done, 1)
                act.wait_ge(ksum_done, done(n, 1))
                act.wait_ge(kinv_done, done(n, 0))
                nc.scalar.activation(knorm[:], ksum[:], ACT.Sqrt).then_inc(knorm_done, 1)
                for b in range(4):
                    act.wait_ge(vb_done, done(n, b // 2 + 1, 2))
                    act.wait_ge(b_put, done(n, 2 * (b // 2) + 2, 4))
                    if b == 0:
                        act.wait_ge(rest1, done(n, 0))
                    nc.scalar.copy(vb[:, :, 0, b], vbp[:, b % 2, 0:256].rearrange("p (q c) -> p q c", q=4)).then_inc(v_put, 1)
                    if b == 1:
                        act.wait_ge(q_done, done(n, 1))
                        act.wait_ge(q_stored, done(n, 0, 16))
                        nc.scalar.copy(q_out[:].rearrange("p (b f) t -> p f b t", f=2),
                                       turned[:].rearrange("p f (b t) -> p f b t", b=4)).then_inc(q_put, 1)
                beta = vb[:, :, 1].rearrange("p q b c -> p q (b c)")
                nc.scalar.activation(beta, beta, ACT.Sigmoid).then_inc(b_sig, 1)
                act.wait_ge(vb_stored, done(n, 0, 16))
                act.wait_ge(v_put, done(n, 4, 4))
                act.wait_ge(b_sig, done(n, 1))
                nc.scalar.copy(parts[:, 0], vb[:].rearrange("p q x b c -> p (q x b c)")).then_inc(part1, 1)
                ahead(1)
                act.wait_ge(rest1, done(n, 1))
                nc.scalar.copy(parts[:, 1], rest[:, 0]).then_inc(part2, 1)

            tiles(act, [deviations, sigmoid], tile)


D = 256
LN_EPS = 1e-5
SLOTS = 256


def done2(n, k=1):
    return n + k + 2


def light_phase(nc, tag, xin, cell, W_out, gamma, w1, b1, w2, b2, token, x2, xr_rows, s_rows):
    T = 512
    with ExitStack() as ctx:
        sb = lambda n, s, d=F32: ctx.enter_context(nc.sbuf_tensor(tag + n, s, d))
        ps = lambda n, s: ctx.enter_context(nc.psum_tensor(tag + n, s, F32))
        sem = phase_semaphores(nc, ctx, tag + "s_")
        ident = sb("ident", [P, P])
        wo_stage = sb("wo_stage", [P, 2, 256])
        wo = sb("wo", [P, 2, 256])
        w1_raw = sb("w1_raw", [P, 2, 128])
        w1g = sb("w1g", [P, 2, 128])
        gam = sb("gam", [P, 2])
        b1c = sb("b1c", [P, 1])
        w2s = sb("w2s", [P, 256])
        b2r = sb("b2r", [P, 256])
        tok = sb("tok", [P, 256])
        eps = sb("eps", [P, 1])
        xt = sb("xt", [P, 2, 4, 256])
        ot = sb("ot", [P, 2, 4, 256])
        sig = sb("sig", [P, 4, 256])
        osq = sb("osq", [P, 4, 256])
        oo = sb("oo", [P, 4, 256])
        oT = sb("oT", [P, 2, 512])
        stats = sb("stats", [P, 4, 6])
        mv = sb("mv", [P, 4, 2])
        std = sb("std", [P, 2, 4])
        rstd = sb("rstd", [P, 4])
        norm = sb("norm", [P, 4])
        normc = sb("normc", [P, 4])
        inv = sb("inv", [P, 4])
        inv16 = sb("inv16", [P, 4])
        rscale = sb("rscale", [P, 4])
        xr = sb("xr", [P, 2, 4, 256])
        prod = sb("prod", [P, 4, 256])
        dot = sb("dot", [P, 4])
        dotn = sb("dotn", [P, 4])
        ss = sb("ss", [P, 4, NB])
        xrT = sb("xrT", [P, 2, 512])
        hid = sb("hid", [P, 512])
        xb = sb("xb", [P, 4, 256])
        xo = sb("xo", [P, 2, 4, 256])
        s_out = sb("s_out", [NB, 512])
        pa = ps("pa", [P, 2, 512])
        pb = ps("pb", [P, 4, 256])
        pc = ps("pc", [P, 512])
        pd = ps("pd", [P, 4, 256])

        id0, id_ready, eps_ready, w_loaded, w_turned, w_put, w1_ready = map(
            sem, ("id0", "id1", "eps", "w", "wturn", "wput", "w1"))
        x_loaded = [sem(f"x{e}") for e in (0, 1)]
        o_loaded = [sem(f"o{e}") for e in (0, 1)]
        sig_done, osq_done, oo_done, o_turned, oT_done, y_done, x1_done = map(
            sem, ("sig", "osq", "oo", "oturn", "oT", "y", "xplus"))
        st_done, ag_done, std_done, r1, r2, r3, r4, r5, r6, xr_done = map(
            sem, ("st", "ag", "std", "r1", "r2", "r3", "r4", "r5", "r6", "xr"))
        prod_done, dot_done, dotn_done, ss_done, xr_turned, xrT_done, h_done, gelu_done, light_done, xb_done, x2_done = map(
            sem, ("prod", "dot", "dotn", "ss", "xrt", "xrT", "h", "gelu", "light", "xb", "x2"))
        x2_stored, xr_stored, dpass, s_turned, s_put, s_stored = map(sem, ("x2st", "xrst", "dpass", "sturn", "sput", "sst"))
        block = ctx.enter_context(nc.Block())
        WLOADS = 16 * (10 if cell is not None else 6)

        def tiles(eng, starts, body):
            for start in starts:
                start(0, 0, 0)
            with eng.Fori(0, NB // 2 - 1) as m:
                body(m * 2, 0, lambda k: starts[k](m * 2 + 1, 1, m))
                body(m * 2 + 1, 1, lambda k: starts[k](m * 2 + 2, 0, m + 1))
            body(NB - 2, 0, lambda k: starts[k](NB - 1, 1, NB // 2 - 1))
            body(NB - 1, 1, lambda k: None)

        @block.sync
        def _(sp):
            with nc.allow_non_contiguous_dma(reason="small constants"):
                sp.dma_start(w1_raw[:], w1.rearrange("(k p) m -> p k m", p=P)).then_inc(w_loaded, 16)
                sp.dma_start(gam[:], gamma.rearrange("(k p) -> p k", p=P)).then_inc(w_loaded, 16)
                sp.dma_start(b1c[:], b1.rearrange("(p o) -> p o", o=1)).then_inc(w_loaded, 16)
                sp.dma_start(w2s[:], w2).then_inc(w_loaded, 16)
                sp.dma_start(b2r[:], b2.partition_broadcast(P)).then_inc(w_loaded, 16)
                sp.dma_start(tok[:], token.partition_broadcast(P)).then_inc(w_loaded, 16)
                if cell is not None:
                    src = W_out.rearrange("(r p) (f q i) -> r f p q i", p=P, f=2, q=4)
                    for r in range(2):
                        for f in range(2):
                            dst = wo_stage[:, r].rearrange("p (q f i) -> p q f i", q=4, f=2)[:, :, f]
                            sp.dma_start(dst, src[r, f]).then_inc(w_loaded, 16)

            def load_cell(n, e):
                if cell is not None:
                    sp.wait_ge(oo_done, done2(n, -1))
                    for t in range(4):
                        src = cell[t * P + U + 1:t * P + P + U + 1, bass.ds(n // 8, 1), :, bass.ds(n % 8 * 64, 64)]
                        sp.dma_start(ot[:, e, t].rearrange("p (q c) -> p q c", q=4),
                                     src.rearrange("t z q c -> t (z q) c")).then_inc(o_loaded[e], 16)

            def load_x(n, e):
                sp.wait_ge(x2_done, done2(n, -1))
                sp.dma_start(xt[:, e], xin[bass.ds(n, 1)].rearrange("o (b p) d -> p (o b) d", p=P)).then_inc(x_loaded[e], 16)

            def store(n, e):
                sp.wait_ge(xr_done, done(n, 4, 4))
                sp.dma_start(xr_rows[bass.ds(n * T, T), :].rearrange("(b p) d -> p b d", p=P), xr[:, e]).then_inc(xr_stored, 16)
                sp.wait_ge(x2_done, done2(n, 1))
                sp.dma_start(x2[bass.ds(n * T, T), :].rearrange("(b p) d -> p b d", p=P), xo[:, e]).then_inc(x2_stored, 16)

            credit(sp, [(x2_stored, 32), (xr_stored, 32)])
            with nc.allow_non_contiguous_dma(reason="runs of 256 bytes"):
                for n in (0, 1):
                    load_cell(n, n)
                    load_x(n, n)
                with sp.Fori(0, NB // 2 - 1) as m:
                    for e in (0, 1):
                        load_cell(m * 2 + e + 2, e)
                        store(m * 2 + e, e)
                        load_x(m * 2 + e + 2, e)
                store(NB - 2, 0)
                store(NB - 1, 1)
            sp.wait_ge(s_put, 1)
            sp.dma_start(s_rows, s_out[:]).then_inc(s_stored, 16)
            sp.wait_ge(s_stored, 16)
            sp.wait_ge(x2_stored, 16 * NB + 32)
            sp.wait_ge(xr_stored, 16 * NB + 32)

        @block.gpsimd
        def _(pool):
            make_identity(nc, ident, id0, id_ready)
            pool.wait_ge(w_loaded, WLOADS)
            credit(pool, [(osq_done, 1), (prod_done, 1), (xb_done, 1)])

            def square(n, e, m):
                if cell is not None:
                    pool.wait_ge(o_loaded[e], m * 64 + 64)
                    pool.wait_ge(oo_done, done2(n, 0))
                    nc.gpsimd.tensor_tensor(osq[:], ot[:, e], ot[:, e], ALU.mult).then_inc(osq_done, 1)

            def tile(n, e, ahead):
                ahead(0)
                pool.wait_ge(xr_done, done(n, 4, 4))
                pool.wait_ge(dot_done, done(n, 0))
                nc.gpsimd.tensor_tensor(prod[:], xr[:, e], tok[:].unsqueeze(1).to_broadcast([P, 4, 256]), ALU.mult).then_inc(prod_done, 1)
                pool.wait_ge(x2_done, done2(n, 0))
                nc.gpsimd.tensor_tensor(xb[:], xt[:, e], b2r[:].unsqueeze(1).to_broadcast([P, 4, 256]), ALU.add).then_inc(xb_done, 1)

            tiles(pool, [square], tile)

        @block.tensor
        def _(pe):
            pe.wait_ge(id_ready, 1)
            if cell is not None:
                pe.wait_ge(w_loaded, WLOADS)
                for k in range(2):
                    for r in range(2):
                        mm = nc.tensor.transpose(pa[:, k, r * P:r * P + P], wo_stage[:, r, k * P:k * P + P], ident[:])
                mm.then_inc(w_turned, 1)
                pe.wait_ge(w_put, 1)
            pe.wait_ge(w1_ready, 2)
            credit(pe, [(o_turned, 1), (y_done, 1), (xr_turned, 1), (h_done, 1), (light_done, 1)])

            def output_layer(n, e, m):
                if cell is not None:
                    pe.wait_ge(xrT_done, done(n, 0))
                    pe.wait_ge(oo_done, done2(n, 1))
                    for t in range(4):
                        for k in range(2):
                            mm = nc.tensor.transpose(pa[:, k, t * P:t * P + P], oo[:, t, k * P:k * P + P], ident[:])
                    mm.then_inc(o_turned, 1)
                    pe.wait_ge(oT_done, done(n, 1))
                    pe.wait_ge(x1_done, done(n, 0))
                    for t in range(4):
                        for k in range(2):
                            mm = nc.tensor.matmul(pb[:, t], oT[:, k, t * P:t * P + P], wo[:, k], start=(k == 0), stop=(k == 1))
                    mm.then_inc(y_done, 1)

            def tile(n, e, ahead):
                pe.wait_ge(xr_done, done(n, 4, 4))
                pe.wait_ge(xrT_done, done(n, 0))
                for t in range(4):
                    for k in range(2):
                        mm = nc.tensor.transpose(pa[:, k, t * P:t * P + P], xr[:, e, t, k * P:k * P + P], ident[:])
                mm.then_inc(xr_turned, 1)
                pe.wait_ge(xrT_done, done(n, 1))
                pe.wait_ge(gelu_done, done(n, 0))
                for k in range(2):
                    mm = nc.tensor.matmul(pc[:], w1g[:, k], xrT[:, k], start=(k == 0), stop=(k == 1))
                mm.then_inc(h_done, 1)
                ahead(0)
                pe.wait_ge(gelu_done, done(n, 1))
                pe.wait_ge(x2_done, done2(n, 0))
                for t in range(4):
                    mm = nc.tensor.matmul(pd[:, t], hid[:, t * P:t * P + P], w2s[:], start=True, stop=True)
                mm.then_inc(light_done, 1)

            tiles(pe, [output_layer], tile)
            pe.wait_ge(ss_done, NB + 1)
            for t in range(4):
                mm = nc.tensor.transpose(pc[0:NB, t * P:t * P + P], ss[:, t], ident[:])
            mm.then_inc(s_turned, 1)

        @block.vector
        def _(dve):
            nc.vector.memset(eps[:], LN_EPS).then_inc(eps_ready, 1)
            dve.wait_ge(w_loaded, WLOADS)
            for k in range(2):
                nc.vector.tensor_scalar(w1g[:, k], w1_raw[:, k], gam[:, k:k + 1], None, ALU.mult).then_inc(w1_ready, 1)
            if cell is not None:
                dve.wait_ge(w_turned, 1)
                nc.vector.tensor_copy(wo[:], pa[:, :, 0:256]).then_inc(w_put, 1)
            credit(dve, [(oo_done, 2), (x1_done, 1), (st_done, 4), (ag_done, 4), (r1, 1), (r2, 1), (r3, 1), (r4, 1), (r5, 1), (r6, 1),
                         (xr_done, 4), (dot_done, 1), (dotn_done, 1), (ss_done, 1), (x2_done, 2)])

            def silu_square(n, e, m):
                if cell is not None:
                    dve.wait_ge(sig_done, done(n, 1))
                    dve.wait_ge(osq_done, done(n, 1))
                    dve.wait_ge(o_turned, done(n, 0))
                    nc.vector.tensor_tensor(oo[:], osq[:], sig[:], ALU.mult).then_inc(oo_done, 1)

            def normalise(n, e, m):
                dve.wait_ge(x_loaded[e], m * 16 + 16)
                if cell is not None:
                    dve.wait_ge(y_done, done(n, 1))
                    nc.vector.tensor_tensor(xt[:, e], xt[:, e], pb[:], ALU.add).then_inc(x1_done, 1)
                    dve.wait_ge(x1_done, done(n, 1))
                for t in range(4):
                    nc.vector.bn_stats(stats[:, t], xt[:, e, t]).then_inc(st_done, 1)
                for t in range(4):
                    dve.wait_ge(st_done, done(n, t + 1, 4))
                    dve.sem_inc(dpass, 1)
                    nc.vector.bn_aggr(mv[:, t], stats[:, t]).then_inc(ag_done, 1)
                dve.wait_ge(std_done, done(n, 2, 2))
                nc.vector.reciprocal(rstd[:], std[:, 1]).then_inc(r1, 1)
                dve.wait_ge(r1, done(n, 1))
                nc.vector.tensor_tensor(norm[:], std[:, 0], rstd[:], ALU.mult).then_inc(r2, 1)
                dve.wait_ge(r2, done(n, 1))
                nc.vector.tensor_scalar(normc[:], norm[:], 16.0, 1e-12, ALU.mult, ALU.max).then_inc(r3, 1)
                dve.wait_ge(r3, done(n, 1))
                nc.vector.reciprocal(inv[:], normc[:]).then_inc(r4, 1)
                dve.wait_ge(r4, done(n, 1))
                nc.vector.tensor_scalar(inv16[:], inv[:], 16.0, None, ALU.mult).then_inc(r5, 1)
                dve.wait_ge(r5, done(n, 1))
                nc.vector.tensor_tensor(rscale[:], inv16[:], rstd[:], ALU.mult).then_inc(r6, 1)
                dve.wait_ge(r6, done(n, 1))
                dve.wait_ge(xr_stored, n * 16 + 16)
                for t in range(4):
                    nc.vector.tensor_scalar(xr[:, e, t], xt[:, e, t], mv[:, t, 0:1], rscale[:, t:t + 1], ALU.subtract, ALU.mult
                                            ).then_inc(xr_done, 1)

            def tile(n, e, ahead):
                ahead(0)
                dve.wait_ge(prod_done, done(n, 1))
                nc.vector.tensor_reduce(dot[:], prod[:], AX_X, ALU.add).then_inc(dot_done, 1)
                dve.wait_ge(dot_done, done(n, 1))
                nc.vector.tensor_tensor(dotn[:], dot[:], normc[:], ALU.mult).then_inc(dotn_done, 1)
                dve.wait_ge(dotn_done, done(n, 1))
                nc.vector.tensor_scalar(ss[:, :, bass.ds(n, 1)], dotn[:].unsqueeze(2), 1 / 16.0, None, ALU.mult).then_inc(ss_done, 1)
                ahead(1)
                dve.wait_ge(light_done, done(n, 1))
                dve.wait_ge(xb_done, done(n, 1))
                dve.wait_ge(x2_stored, n * 16 + 16)
                nc.vector.tensor_tensor(xo[:, e], xb[:], pd[:], ALU.add).then_inc(x2_done, 1)

            tiles(dve, [silu_square, normalise], tile)
            dve.wait_ge(s_turned, 1)
            nc.vector.tensor_copy(s_out[:], pc[0:NB, :]).then_inc(s_put, 1)

        @block.scalar
        def _(act):
            act.wait_ge(eps_ready, 1)
            act.wait_ge(w_loaded, WLOADS)
            credit(act, [(sig_done, 1), (oT_done, 1), (std_done, 2), (xrT_done, 1), (gelu_done, 1)])

            def sigmoid(n, e, m):
                if cell is not None:
                    act.wait_ge(o_loaded[e], m * 64 + 64)
                    act.wait_ge(oo_done, done2(n, 0))
                    nc.scalar.activation(sig[:], ot[:, e], ACT.Sigmoid).then_inc(sig_done, 1)

            def deviations(n, e, m):
                if cell is not None:
                    act.wait_ge(o_turned, done(n, 1))
                    act.wait_ge(y_done, done(n, 0))
                    nc.scalar.copy(oT[:], pa[:]).then_inc(oT_done, 1)
                act.wait_ge(ag_done, done(n, 4, 4))
                act.wait_ge(r2, done(n, 0))
                nc.scalar.activation(std[:, 0], mv[:, :, 1], ACT.Sqrt).then_inc(std_done, 1)
                nc.scalar.activation(std[:, 1], mv[:, :, 1], ACT.Sqrt, bias=eps[:]).then_inc(std_done, 1)

            def tile(n, e, ahead):
                ahead(0)
                act.wait_ge(xr_turned, done(n, 1))
                act.wait_ge(h_done, done(n, 0))
                nc.scalar.copy(xrT[:], pa[:]).then_inc(xrT_done, 1)
                act.wait_ge(h_done, done(n, 1))
                act.wait_ge(light_done, done(n, 0))
                nc.scalar.activation(hid[:], pc[:], ACT.Gelu, bias=b1c[:]).then_inc(gelu_done, 1)
                ahead(1)

            tiles(act, [sigmoid, deviations], tile)



I32 = mybir.dt.int32


def router_phase(nc, tag, s_rows, lidx, lgate):
    T, ITERS, KEEP = 512, 50, SLOTS * 9.0 / 8.0
    with ExitStack() as ctx:
        sb = lambda n, s, d=F32: ctx.enter_context(nc.sbuf_tensor(tag + n, s, d))
        ps = lambda n, s: ctx.enter_context(nc.psum_tensor(tag + n, s, F32))
        sem = phase_semaphores(nc, ctx, tag + "s_")
        ident = sb("ident", [P, P])
        s = sb("s", [NB, T])
        sb_ = sb("sb_", [NB, T])
        ex = sb("ex", [NB, T])
        smax = sb("smax", [NB, 1])
        na = sb("na", [NB, 1])
        nm = sb("nm", [NB, 1])
        tot = sb("tot", [NB, 1])
        lg = sb("lg", [NB, 1])
        z = sb("z", [NB, T])
        score = sb("score", [NB, T])
        work = sb("work", [NB, T])
        top = sb("top", [NB, 8])
        mask = sb("mask", [NB, T])
        comp = sb("comp", [NB, T])
        gate = sb("gate", [NB, T])
        upto = sb("upto", [P, P])
        ones = sb("ones", [P, P])
        slot_no = sb("slot_no", [P, SLOTS])
        maskT = sb("maskT", [P, 4, NB])
        vals = sb("vals", [P, 4, NB, 2])
        pm = sb("pm", [P, 4, NB])
        slot = sb("slot", [P, 4, NB])
        hot = sb("hot", [P, 2, 4, SLOTS])
        idx = sb("idx", [P, 2 * NB], I32)
        gates = sb("gates", [P, 2 * NB])
        pt = ps("pt", [P, 2, 4 * NB])
        pp = ps("pp", [P, 4, NB])
        pl = ps("pl", [P, NB, 2, 2])
        loaded, id0, id_ready, c_ready, made = map(sem, ("ld", "id0", "id1", "c", "made"))
        max_done, sb_done, nm_done, ex_done, ln_done, na_done, z_done, score_done = map(
            sem, ("max", "sb", "nm", "ex", "ln", "na", "z", "sc"))
        work_done, top_done, mask_done, comp_done, gate_done, turned, mT, vT, pos_done, pm_done, slot_done = map(
            sem, ("work", "top", "mask", "comp", "gate", "turn", "mT", "vT", "pos", "pm", "slot"))
        hot_done, list_done, idx_done, stored = map(sem, ("hot", "list", "idx", "st"))
        block = ctx.enter_context(nc.Block())

        @block.sync
        def _(sp):
            sp.dma_start(s[:], s_rows).then_inc(loaded, 16)
            sp.wait_ge(idx_done, 2)
            sp.dma_start(lidx, idx[:]).then_inc(stored, 16)
            sp.dma_start(lgate, gates[:]).then_inc(stored, 16)
            sp.wait_ge(stored, 32)

        @block.gpsimd
        def _(pool):
            make_identity(nc, ident, id0, id_ready)
            nc.gpsimd.memset(ones[:], 1.0).then_inc(made, 1)
            pool.wait_ge(made, 1)
            nc.gpsimd.affine_select(out=upto[:], in_=ones[:], compare_op=ALU.is_ge, fill=0.0, base=0,
                                    pattern=[[1, P]], channel_multiplier=-1).then_inc(c_ready, 1)
            nc.gpsimd.iota(slot_no[:], pattern=[[1, SLOTS]], base=0, channel_multiplier=0,
                           allow_small_or_imprecise_dtypes=True).then_inc(c_ready, 1)
            for t in range(4):
                nc.gpsimd.iota(vals[:, t, :, 0], pattern=[[T, NB]], base=t * P, channel_multiplier=1,
                               allow_small_or_imprecise_dtypes=True).then_inc(c_ready, 1)

        @block.tensor
        def _(pe):
            pe.wait_ge(id_ready, 1)
            pe.wait_ge(mask_done, 1)
            pe.wait_ge(gate_done, 1)
            for x, src in enumerate((mask, gate)):
                for t in range(4):
                    mm = nc.tensor.transpose(pt[:, x, t * NB:t * NB + NB], src[:, t * P:t * P + P], ident[0:NB, 0:NB])
            mm.then_inc(turned, 1)
            pe.wait_ge(mT, 1)
            pe.wait_ge(c_ready, 6)
            for t in range(4):
                for t2 in range(t + 1):
                    mm = nc.tensor.matmul(pp[:, t], (upto if t2 == t else ones)[:], maskT[:, t2], start=(t2 == 0), stop=(t2 == t))
            mm.then_inc(pos_done, 1)
            pe.wait_ge(vT, 1)
            pe.sem_inc(list_done, 2)
            with pe.Fori(0, NB // 2) as m:
                for e in (0, 1):
                    b = m * 2 + e
                    pe.wait_ge(hot_done, b * 4 + 4)
                    for h in range(2):
                        for t in range(4):
                            mm = nc.tensor.matmul(pl[:, bass.ds(b, 1), h, :], hot[:, e, t, h * P:h * P + P],
                                                  vals[:, t, bass.ds(b, 1), :], start=(t == 0), stop=(t == 3))
                    mm.then_inc(list_done, 1)

        @block.vector
        def _(dve):
            dve.wait_ge(loaded, 16)
            nc.vector.tensor_reduce(smax[:], s[:], AX_X, ALU.max).then_inc(max_done, 1)
            nc.vector.memset(na[:], math.log(T) - math.log(KEEP)).then_inc(na_done, 1)
            dve.wait_ge(max_done, 1)
            with dve.Fori(0, ITERS - 1) as k:
                dve.wait_ge(na_done, k + 1)
                nc.vector.tensor_scalar(nm[:], smax[:], na[:], -1.0, ALU.min, ALU.mult).then_inc(nm_done, 1)
                nc.vector.tensor_scalar(sb_[:], s[:], na[:], None, ALU.min).then_inc(sb_done, 1)
                dve.wait_ge(ln_done, k + 1)
                nc.vector.tensor_scalar(na[:], lg[:], math.log(KEEP), nm[:], ALU.subtract, ALU.subtract).then_inc(na_done, 1)
            dve.wait_ge(na_done, ITERS)
            nc.vector.tensor_scalar(z[:], s[:], na[:], 0.0, ALU.subtract, ALU.min).then_inc(z_done, 1)
            dve.wait_ge(score_done, 1)
            nc.vector.tensor_copy(work[:], score[:]).then_inc(work_done, 1)
            nc.vector.tensor_scalar(comp[:], score[:], -1.0, 1.0, ALU.mult, ALU.add).then_inc(comp_done, 1)
            dve.wait_ge(comp_done, 1)
            nc.vector.tensor_tensor(gate[:], score[:], comp[:], ALU.add).then_inc(gate_done, 1)
            for r in range(SLOTS // 8):
                dve.wait_ge(work_done, r + 1)
                nc.vector.max(top[:], work[:]).then_inc(top_done, 1)
                dve.wait_ge(top_done, r + 1)
                nc.vector.match_replace(work[:], top[:], work[:], -1.0).then_inc(work_done, 1)
            dve.wait_ge(work_done, SLOTS // 8 + 1)
            nc.vector.tensor_scalar(mask[:], work[:], 0.0, None, ALU.is_lt).then_inc(mask_done, 1)
            dve.wait_ge(turned, 1)
            nc.vector.tensor_copy(maskT[:], pt[:, 0].rearrange("p (t b) -> p t b", t=4)).then_inc(mT, 1)
            dve.wait_ge(c_ready, 6)
            nc.vector.tensor_copy(vals[:, :, :, 1], pt[:, 1].rearrange("p (t b) -> p t b", t=4)).then_inc(vT, 1)
            dve.wait_ge(mT, 1)
            dve.wait_ge(pos_done, 1)
            nc.vector.tensor_tensor(pm[:], pp[:], maskT[:], ALU.mult).then_inc(pm_done, 1)
            dve.wait_ge(pm_done, 1)
            nc.vector.tensor_scalar(slot[:], pm[:], -1.0, None, ALU.add).then_inc(slot_done, 1)
            dve.wait_ge(slot_done, 1)
            with dve.Fori(0, NB // 2) as m:
                for e in (0, 1):
                    b = m * 2 + e
                    dve.wait_ge(list_done, b + 1)
                    for t in range(4):
                        nc.vector.tensor_scalar(hot[:, e, t], slot_no[:], slot[:, t, bass.ds(b, 1)], None, ALU.is_equal).then_inc(hot_done, 1)
            dve.wait_ge(list_done, NB + 2)
            nc.vector.tensor_copy(idx[:], pl[:, :, :, 0].rearrange("p b h -> p (b h)")).then_inc(idx_done, 1)
            nc.vector.tensor_copy(gates[:], pl[:, :, :, 1].rearrange("p b h -> p (b h)")).then_inc(idx_done, 1)

        @block.scalar
        def _(act):
            nc.scalar.preload_act_table_set("natural_log_exp_and_others")
            with act.Fori(0, ITERS - 1) as k:
                act.wait_ge(sb_done, k + 1)
                act.wait_ge(nm_done, k + 1)
                nc.scalar.activation(ex[:], sb_[:], ACT.Exp, bias=nm[:], accum_out=tot[:]).then_inc(ex_done, 1)
                act.wait_ge(ex_done, k + 1)
                nc.scalar.activation(lg[:], tot[:], ACT.Ln).then_inc(ln_done, 1)
            act.wait_ge(z_done, 1)
            nc.scalar.activation(score[:], z[:], ACT.Exp).then_inc(score_done, 1)


def heavy_phase(nc, tag, xr_rows, x2, lidx, lgate, gamma, w1, b1, w2, b2):
    HID = 1024
    C, TILES = HID // P, 2 * NB // 4
    with ExitStack() as ctx:
        sb = lambda n, s, d=F32: ctx.enter_context(nc.sbuf_tensor(tag + n, s, d))
        ps = lambda n, s: ctx.enter_context(nc.psum_tensor(tag + n, s, F32))
        sem = phase_semaphores(nc, ctx, tag + "s_")
        ident = sb("ident", [P, P])
        w1_raw = sb("w1_raw", [P, 2, HID])
        w1g = sb("w1g", [P, 2, HID])
        gam = sb("gam", [P, 2])
        b1c = sb("b1c", [P, C])
        w2s = sb("w2s", [P, C, 256])
        b2r = sb("b2r", [P, 256])
        idx = sb("idx", [P, 2 * NB], I32)
        gates = sb("gates", [P, 2 * NB])
        cur = sb("cur", [P, 2, 4], I32)
        curg = sb("curg", [P, 2, 4])
        xg = sb("xg", [P, 2, 4, 256])
        xo = sb("xo", [P, 2, 4, 256])
        xgT = sb("xgT", [P, 2, 512])
        hid = sb("hid", [P, C, 512])
        yb = sb("yb", [P, 4, 256])
        res = sb("res", [P, 2, 4, 256])
        pa = ps("pa", [P, 2, 512])
        ph = ps("ph", [P, 2, 512])
        py = ps("py", [P, 4, 256])
        w_loaded, id0, id_ready, w1_ready = map(sem, ("w", "id0", "id1", "w1g"))
        cur_done, turned, xgT_done, h_done, gelu_done, y_done, yb_done, res_done = map(
            sem, ("cur", "turn", "xgT", "h", "gelu", "y", "yb", "res"))
        passed = sem("pass")
        fetched = [sem(f"f{e}") for e in (0, 1)]
        put = [sem(f"put{e}") for e in (0, 1)]
        block = ctx.enter_context(nc.Block())

        def tiles(eng, body, start=None):
            if start:
                start(0, 0, 0)
            with eng.Fori(0, TILES // 2 - 1) as m:
                body(m * 2, 0, lambda: start(m * 2 + 1, 1, m))
                body(m * 2 + 1, 1, lambda: start(m * 2 + 2, 0, m + 1))
            body(TILES - 2, 0, lambda: start(TILES - 1, 1, TILES // 2 - 1))
            body(TILES - 1, 1, lambda: None)

        @block.sync
        def _(sp):
            with nc.allow_non_contiguous_dma(reason="small constants"):
                sp.dma_start(w1_raw[:], w1.rearrange("(k p) m -> p k m", p=P)).then_inc(w_loaded, 16)
                sp.dma_start(gam[:], gamma.rearrange("(k p) -> p k", p=P)).then_inc(w_loaded, 16)
                sp.dma_start(b1c[:], b1.rearrange("(c p) -> p c", p=P)).then_inc(w_loaded, 16)
                sp.dma_start(w2s[:], w2.rearrange("(c p) d -> p c d", p=P)).then_inc(w_loaded, 16)
                sp.dma_start(b2r[:], b2.partition_broadcast(P)).then_inc(w_loaded, 16)
                sp.dma_start(idx[:], lidx).then_inc(w_loaded, 16)
                sp.dma_start(gates[:], lgate).then_inc(w_loaded, 16)

        @block.gpsimd
        def _(pool):
            make_identity(nc, ident, id0, id_ready)

            def fetch(n, e):
                pool.wait_ge(cur_done, done(n, 2, 2))
                pool.wait_ge(turned, n + 1)
                pool.wait_ge(res_done, n * 4 + 4)
                pool.sem_inc(passed, 1)
                for dst, src in ((xg, xr_rows), (xo, x2)):
                    for j in range(4):
                        nc.gpsimd.indirect_dma_start(out=dst[:, e, j], out_offset=None, in_=src,
                                                     in_offset=bass.IndirectOffsetOnAxis(ap=cur[:, e, j:j + 1], axis=0)
                                                     ).then_inc(fetched[e], 16)

            def scatter(n, e):
                pool.wait_ge(res_done, n * 4 + 12)
                pool.sem_inc(passed, 1)
                for j in range(4):
                    nc.gpsimd.indirect_dma_start(out=x2, out_offset=bass.IndirectOffsetOnAxis(ap=cur[:, e, j:j + 1], axis=0),
                                                 in_=res[:, e, j], in_offset=None).then_inc(put[e], 16)

            fetch(0, 0)
            with pool.Fori(0, TILES // 2 - 1) as m:
                for e in (0, 1):
                    fetch(m * 2 + 1 + e, 1 - e)
                    scatter(m * 2 + e, e)
            fetch(TILES - 1, 1)
            scatter(TILES - 2, 0)
            scatter(TILES - 1, 1)
            for e in (0, 1):
                pool.wait_ge(put[e], 64 * TILES // 2)

        @block.tensor
        def _(pe):
            pe.wait_ge(id_ready, 1)
            pe.wait_ge(w1_ready, 2)
            credit(pe, [(turned, 2), (h_done, C), (y_done, 1)])

            def turn(n, e, m):
                pe.wait_ge(fetched[e], m * 128 + 128)
                pe.wait_ge(xgT_done, n + 1)
                for t in range(4):
                    for k in range(2):
                        mm = nc.tensor.transpose(pa[:, k, t * P:t * P + P], xg[:, e, t, k * P:k * P + P], ident[:])
                mm.then_inc(turned, 1)

            def tile(n, e, ahead):
                pe.wait_ge(xgT_done, n + 2)
                for c in range(C):
                    pe.wait_ge(gelu_done, n * C + C + c - 1)
                    for k in range(2):
                        mm = nc.tensor.matmul(ph[:, c % 2], w1g[:, k, c * P:c * P + P], xgT[:, k], start=(k == 0), stop=(k == 1))
                    mm.then_inc(h_done, 1)
                ahead()
                pe.wait_ge(yb_done, n + 1)
                for t in range(4):
                    for c in range(C):
                        if t == 0:
                            pe.wait_ge(gelu_done, n * C + C + c + 1)
                        mm = nc.tensor.matmul(py[:, t], hid[:, c, t * P:t * P + P], w2s[:, c], start=(c == 0), stop=(c == C - 1))
                mm.then_inc(y_done, 1)

            tiles(pe, tile, turn)

        @block.vector
        def _(dve):
            dve.wait_ge(w_loaded, 16 * 7)
            for k in range(2):
                nc.vector.tensor_scalar(w1g[:, k], w1_raw[:, k], gam[:, k:k + 1], None, ALU.mult).then_inc(w1_ready, 1)
            credit(dve, [(cur_done, 2), (yb_done, 1), (res_done, 8)])

            def pick(n, e):
                nc.vector.tensor_copy(cur[:, e], idx[:, bass.ds(n * 4, 4)]).then_inc(cur_done, 1)
                nc.vector.tensor_copy(curg[:, e], gates[:, bass.ds(n * 4, 4)]).then_inc(cur_done, 1)

            def tile(n, e):
                dve.wait_ge(y_done, n + 2)
                dve.wait_ge(res_done, n * 4 + 8)
                nc.vector.tensor_tensor(yb[:], py[:], b2r[:].unsqueeze(1).to_broadcast([P, 4, 256]), ALU.add).then_inc(yb_done, 1)
                dve.wait_ge(yb_done, n + 2)
                for t in range(4):
                    nc.vector.scalar_tensor_tensor(res[:, e, t], yb[:, t], curg[:, e, t:t + 1], xo[:, e, t], ALU.mult, ALU.add
                                                   ).then_inc(res_done, 1)

            pick(0, 0)
            pick(1, 1)
            with dve.Fori(0, TILES // 2 - 1) as m:
                for e in (0, 1):
                    tile(m * 2 + e, e)
                    dve.wait_ge(put[e], m * 64 + 64)
                    pick(m * 2 + e + 2, e)
            tile(TILES - 2, 0)
            tile(TILES - 1, 1)

        @block.scalar
        def _(act):
            act.wait_ge(w_loaded, 16 * 7)
            credit(act, [(xgT_done, 1), (gelu_done, C)])

            def copy_x(n, e, m):
                act.wait_ge(turned, n + 3)
                act.wait_ge(h_done, n * C + C)
                nc.scalar.copy(xgT[:], pa[:]).then_inc(xgT_done, 1)

            def tile(n, e, ahead):
                for c in range(C):
                    act.wait_ge(h_done, n * C + C + c + 1)
                    if c == 0:
                        act.wait_ge(y_done, n + 1)
                    nc.scalar.activation(hid[:, c], ph[:, c % 2], ACT.Gelu, bias=b1c[:, c:c + 1]).then_inc(gelu_done, 1)
                ahead()

            tiles(act, tile, copy_x)


HEADS, HD = 16, 16
HG = 4


def qkv_phase(nc, tag, xin, Wq, Wk, Wv, qk_parts, v_rows):
    T = 512
    with ExitStack() as ctx:
        sb = lambda n, s, d=F32: ctx.enter_context(nc.sbuf_tensor(tag + n, s, d))
        ps = lambda n, s: ctx.enter_context(nc.psum_tensor(tag + n, s, F32))
        sem = phase_semaphores(nc, ctx, tag + "s_")
        ident = sb("ident", [P, P])
        w = sb("w", [P, 3, 2, 256])
        wq4 = sb("wq4", [P, 2, 256])
        eps = sb("eps", [P, 1])
        xt = sb("xt", [P, 2, 4, 256])
        stats = sb("stats", [P, 4, 6])
        mv = sb("mv", [P, 4, 2])
        std = sb("std", [P, 4])
        rstd = sb("rstd", [P, 4])
        xl = sb("xl", [P, 4, 256])
        xlT = sb("xlT", [P, 2, T])
        parts = sb("parts", [P, 2, 3, 2, T], BF16)
        rest = sb("rest", [P, 2, 2, T])
        vpad = sb("vpad", [P, 4, HEADS, 32])
        pa = ps("pa", [P, 2, T])
        pqk = ps("pqk", [P, 2, 2, T])
        pv = ps("pv", [P, 4, 256])
        id0, id_ready, eps_ready, w_loaded, w_ready, v_zero = map(sem, ("id0", "id1", "eps", "w", "wr", "vz"))
        x_loaded = [sem(f"x{e}") for e in (0, 1)]
        st_done, ag_done, std_done, rstd_done, xl_done, xl_turned, xlT_done, passed = map(
            sem, ("st", "ag", "std", "rstd", "xl", "xlt", "xlT", "pd"))
        qk_done, v_done, p1, rest1, p2, p3, v_put, qk_stored, v_stored = map(
            sem, ("qk", "v", "p1", "r1", "p2", "p3", "vp", "qkst", "vst"))
        block = ctx.enter_context(nc.Block())

        def tiles(eng, start, body):
            start(0, 0)
            with eng.Fori(0, NB // 2 - 1) as m:
                for e in (0, 1):
                    body(m * 2 + e, lambda: start(m * 2 + e + 1, 1 - e))
            body(NB - 2, lambda: start(NB - 1, 1))
            body(NB - 1, lambda: None)

        @block.sync
        def _(sp):
            for x, src in enumerate((Wq, Wk, Wv)):
                sp.dma_start(w[:, x], src.rearrange("(k p) m -> p k m", p=P)).then_inc(w_loaded, 16)
            credit(sp, [(qk_stored, 12 * 16), (v_stored, 16)])

            def load(n, e):
                sp.wait_ge(xl_done, done(n, 0, 4))
                sp.dma_start(xt[:, e], xin[bass.ds(n * T, T), :].rearrange("(b p) d -> p b d", p=P)).then_inc(x_loaded[e], 16)

            def store(n):
                sp.wait_ge(v_put, done(n, 1))
                sp.dma_start(v_rows[bass.ds(n * T, T), :].rearrange("(b p) c -> p b c", p=P),
                             vpad[:].rearrange("p t h d -> p t (h d)")).then_inc(v_stored, 16)
                for x in (0, 1):
                    sp.wait_ge(p3, done(n, x + 1, 2))
                    for part in range(3):
                        for c in range(2):
                            rank = part if x == 0 else 2 - part
                            dst = qk_parts[bass.ds(n, 1), x, 8 * c:8 * c + 8, rank * HD:(rank + 1) * HD, :]
                            sp.dma_start(dst.rearrange("o h d t -> (o h) d t"), parts[:, x, part, c]).then_inc(qk_stored, 16)

            load(0, 0)
            load(1, 1)
            with sp.Fori(0, NB // 2 - 1) as m:
                for e in (0, 1):
                    load(m * 2 + e + 2, e)
                    store(m * 2 + e)
            store(NB - 2)
            store(NB - 1)
            sp.wait_ge(qk_stored, 12 * 16 * (NB + 1))
            sp.wait_ge(v_stored, 16 * (NB + 1))

        @block.gpsimd
        def _(pool):
            make_identity(nc, ident, id0, id_ready)
            nc.gpsimd.memset(vpad[:].rearrange("p t h d -> p (t h d)"), 0.0).then_inc(v_zero, 1)

        @block.tensor
        def _(pe):
            pe.wait_ge(id_ready, 1)
            pe.wait_ge(w_loaded, 48)
            pe.wait_ge(w_ready, 1)
            credit(pe, [(xl_turned, 1), (qk_done, 2), (v_done, 1)])

            def turn(n, e):
                pe.wait_ge(xl_done, done(n, 4, 4) + 4)
                pe.wait_ge(xlT_done, done(n, 0))
                for t in range(4):
                    for k in range(2):
                        mm = nc.tensor.transpose(pa[:, k, t * P:t * P + P], xl[:, t, k * P:k * P + P], ident[:])
                mm.then_inc(xl_turned, 1)

            def tile(n, next_row):
                pe.wait_ge(xlT_done, done(n, 1))
                for x in (0, 1):
                    pe.wait_ge(rest1, done(n, x - 1, 2))
                    for c in range(2):
                        for k in range(2):
                            m = wq4[:, k, c * P:c * P + P] if x == 0 else w[:, 1, k, c * P:c * P + P]
                            mm = nc.tensor.matmul(pqk[:, x, c], m, xlT[:, k], start=(k == 0), stop=(k == 1))
                    mm.then_inc(qk_done, 1)
                pe.wait_ge(v_put, done(n, 0))
                for t in range(4):
                    for k in range(2):
                        mm = nc.tensor.matmul(pv[:, t], xlT[:, k, t * P:t * P + P], w[:, 2, k], start=(k == 0), stop=(k == 1))
                mm.then_inc(v_done, 1)
                next_row()

            tiles(pe, turn, tile)

        @block.vector
        def _(dve):
            nc.vector.memset(eps[:], LN_EPS).then_inc(eps_ready, 1)
            dve.wait_ge(w_loaded, 48)
            nc.vector.tensor_scalar(wq4[:], w[:, 0], 0.25, None, ALU.mult).then_inc(w_ready, 1)
            credit(dve, [(st_done, 4), (ag_done, 4), (rstd_done, 1), (xl_done, 8), (rest1, 2), (p3, 2)])

            def normalise(n, e):
                dve.wait_ge(x_loaded[e], (n - e) * 8 + 16)
                for t in range(4):
                    nc.vector.bn_stats(stats[:, t], xt[:, e, t]).then_inc(st_done, 1)
                for t in range(4):
                    dve.wait_ge(st_done, done(n, t + 1, 4))
                    dve.sem_inc(passed, 1)
                    nc.vector.bn_aggr(mv[:, t], stats[:, t]).then_inc(ag_done, 1)
                dve.wait_ge(std_done, done(n, 1))
                nc.vector.reciprocal(rstd[:], std[:]).then_inc(rstd_done, 1)
                dve.wait_ge(rstd_done, done(n, 1))
                dve.wait_ge(xl_turned, done(n, 0))
                for t in range(4):
                    nc.vector.tensor_scalar(xl[:, t], xt[:, e, t], mv[:, t, 0:1], rstd[:, t:t + 1], ALU.subtract, ALU.mult
                                            ).then_inc(xl_done, 1)

            def tile(n, next_row):
                next_row()
                for x in (0, 1):
                    dve.wait_ge(p1, done(n, x + 1, 2))
                    nc.vector.tensor_tensor(rest[:, x], pqk[:, x], parts[:, x, 0], ALU.subtract).then_inc(rest1, 1)
                for x in (0, 1):
                    dve.wait_ge(p2, done(n, x + 1, 2))
                    nc.vector.tensor_tensor(parts[:, x, 2], rest[:, x], parts[:, x, 1], ALU.subtract).then_inc(p3, 1)

            tiles(dve, normalise, tile)

        @block.scalar
        def _(act):
            act.wait_ge(eps_ready, 1)
            act.wait_ge(v_zero, 1)
            credit(act, [(std_done, 1), (xlT_done, 1), (p1, 2), (p2, 2), (v_put, 1)])

            def deviations(n, e):
                act.wait_ge(ag_done, done(n, 4, 4))
                act.wait_ge(rstd_done, done(n, 0))
                nc.scalar.activation(std[:], mv[:, :, 1], ACT.Sqrt, bias=eps[:]).then_inc(std_done, 1)

            def tile(n, next_row):
                act.wait_ge(xl_turned, done(n, 1))
                act.wait_ge(v_done, done(n, 0))
                nc.scalar.copy(xlT[:], pa[:]).then_inc(xlT_done, 1)
                next_row()
                act.wait_ge(qk_stored, done(n, 0, 12 * 16))
                for x in (0, 1):
                    act.wait_ge(qk_done, done(n, x + 1, 2))
                    nc.scalar.copy(parts[:, x, 0], pqk[:, x]).then_inc(p1, 1)
                for x in (0, 1):
                    act.wait_ge(rest1, done(n, x + 1, 2))
                    nc.scalar.copy(parts[:, x, 1], rest[:, x]).then_inc(p2, 1)
                act.wait_ge(v_done, done(n, 1))
                act.wait_ge(v_stored, done(n, 0, 16))
                nc.scalar.copy(vpad[:, :, :, 0:HD], pv[:].rearrange("p t (h d) -> p t h d", h=HEADS)).then_inc(v_put, 1)

            tiles(act, deviations, tile)


def attention_phase(nc, tag, xin, qk_parts, v_rows, xout):
    T, G, UN = 512, HEADS // HG, 16
    with ExitStack() as ctx:
        sb = lambda n, s, d=F32: ctx.enter_context(nc.sbuf_tensor(tag + n, s, d))
        ps = lambda n, s: ctx.enter_context(nc.psum_tensor(tag + n, s, F32))
        sem = phase_semaphores(nc, ctx, tag + "s_")
        ident = sb("ident", [P, P])
        xt = sb("xt", [P, 2, 4, 256])
        qk = sb("qk", [6 * HD, 2, 2, HG, T], BF16)
        v = sb("v", [P, 2, 4, P])
        nmx = sb("nmx", [P, 4])
        al = sb("al", [P, 4, T])
        sums = sb("sums", [P, 4, HG])
        rec = sb("rec", [P, 4, HG])
        alT = sb("alT", [P, 2, 4, T])
        oT = sb("oT", [P, T])
        on = sb("on", [P, 4, HG, HD])
        pscore = ps("score", [P, 4, T])
        pt = ps("pt", [P, 2, 4, P])
        po = ps("po", [P, T])
        pn = ps("pn", [P, 4, P])
        id0, id_ready, passed_p, passed_d = map(sem, ("id0", "id1", "pp", "pd"))
        x_loaded = [sem(f"x{e}") for e in (0, 1)]
        qk_loaded = [sem(f"qk{e}") for e in (0, 1)]
        s_done, mx_done, ex_done, mask_done, t_done, pv_done = map(sem, ("s", "mx", "ex", "mask", "t", "pv"))
        c_dve, c_act = sem("cd"), sem("ca")
        o_put, o_turned, rec_done, norm_done, add_done, stored = map(sem, ("op", "ot", "rec", "norm", "add", "st2"))
        block = ctx.enter_context(nc.Block())
        LOADS = 7 * 16

        def groups(eng, start, group):
            with eng.Fori(0, NB // 2) as m:
                for e in (0, 1):
                    start(m * 2 + e, e, m)
                    with eng.Fori(0, G // 2) as g:
                        for r in (0, 1):
                            group((m * 2 + e) * G + g * 2 + r, g * 2 + r, e, r)

        def copied(eng, i, u):
            h, qb = divmod(u, 4)
            if qb == 3:
                eng.wait_ge(c_act, i * 4 + 4 + h + 1)
            else:
                eng.wait_ge(c_dve, i * 12 + 12 + 3 * h + qb + 1)

        @block.sync
        def _(sp):
            credit(sp, [(stored, 32)])

            def load(n, e):
                sp.wait_ge(stored, n * 16 + 16)
                sp.dma_start(xt[:, e], xin[bass.ds(n * T, T), :].rearrange("(b p) d -> p b d", p=P)).then_inc(x_loaded[e], 16)

            def load_group(i, n, g, r):
                sp.wait_ge(pv_done, i * 4 + 4)
                for x in (0, 1):
                    src = qk_parts[bass.ds(n, 1), x, bass.ds(g * HG, HG)].rearrange("o h r t -> r (o h) t")
                    for row, part, m in ((0, 0, 3), (3, x, 2), (5, 2 * x, 1)):
                        sp.dma_start(qk[row * HD:(row + m) * HD, r, x], src[part * HD:(part + m) * HD]).then_inc(qk_loaded[r], 16)
                sp.dma_start(v[:, r], v_rows[bass.ds(n * T, T), bass.ds(g * P, P)].rearrange("(b p) c -> p b c", p=P)
                             ).then_inc(qk_loaded[r], 16)

            def store(n, e):
                sp.wait_ge(add_done, n * G + G + 1)
                sp.dma_start(xout[bass.ds(n * T, T), :].rearrange("(b p) d -> p b d", p=P), xt[:, e]).then_inc(stored, 16)

            def row(n, e):
                for g in range(G):
                    load_group(n * G + g, n, g, g % 2)
                    if g == 1:
                        if not isinstance(n, int) or n > 0:
                            store(n - 1, 1 - e)
                        if not isinstance(n, int) or n < NB - 1:
                            load(n + 1, 1 - e)

            load(0, 0)
            row(0, 0)
            with sp.Fori(0, NB // 2 - 1) as m:
                row(m * 2 + 1, 1)
                row(m * 2 + 2, 0)
            row(NB - 1, 1)
            load_group(NB * G, 0, 0, 0)
            store(NB - 1, 1)
            sp.wait_ge(stored, 16 * NB + 32)

        @block.gpsimd
        def _(pool):
            make_identity(nc, ident, id0, id_ready)
            credit(pool, [(mask_done, UN)])

            def group(i, g, e, r):
                for u in range(UN):
                    qb = u % 4
                    pool.wait_ge(ex_done, i * UN + UN + u + 1)
                    pool.sem_inc(passed_p, 1)
                    d = al[:, u % 4, qb * P:qb * P + P]
                    nc.gpsimd.affine_select(out=d, in_=d, compare_op=ALU.is_ge, fill=0.0, base=0,
                                            pattern=[[-1, P]], channel_multiplier=1).then_inc(mask_done, 1)

            groups(pool, lambda n, e, m: None, group)

        @block.tensor
        def _(pe):
            pe.wait_ge(id_ready, 1)
            credit(pe, [(s_done, UN), (t_done, UN), (pv_done, 8), (o_turned, 1)])

            def scores(i, r, u):
                h, qb = divmod(u, 4)
                pe.wait_ge(ex_done, i * UN + UN + u - 3)
                nc.tensor.matmul(pscore[:, u % 4], qk[:, r, 0, h, qb * P:qb * P + P], qk[:, r, 1, h, :],
                                 start=True, stop=True).then_inc(s_done, 1)

            def turn(i, u):
                qb = u % 4
                pe.wait_ge(mask_done, i * UN + UN + u + 1)
                if u < 2:
                    copied(pe, i - 1, u + UN - 2)
                else:
                    copied(pe, i, u - 2)
                for kb in range(qb + 1):
                    mm = nc.tensor.transpose(pt[:, u % 2, kb], al[:, u % 4, kb * P:kb * P + P], ident[:])
                mm.then_inc(t_done, 1)

            def values(i, r, h):
                copied(pe, i, 4 * h + 3)
                copied(pe, i, 4 * h + 2)
                if h == 0:
                    pe.wait_ge(o_put, i + 1)
                for kb in range(4):
                    mm = nc.tensor.matmul(po[32 * h:32 * h + 32, kb * P:], v[:, r, kb, 32 * h:32 * h + 32],
                                          alT[:, h % 2, kb, kb * P:], start=(kb == 0), stop=(kb == 3), skip_group_check=True)
                mm.then_inc(pv_done, 1)

            def first_scores(i, r, m):
                pe.wait_ge(qk_loaded[r], m * LOADS + LOADS)
                for u in range(3):
                    scores(i, r, u)

            def group(i, g, e, r):
                for u in range(UN):
                    if u + 3 < UN:
                        scores(i, r, u + 3)
                    turn(i, u)
                    if u % 4 == 2 and u > 4:
                        values(i, r, u // 4 - 1)
                first_scores(i + 1, 1 - r, (i + 1) // 2)
                values(i, r, 3)
                pe.wait_ge(o_put, i + 2)
                pe.wait_ge(norm_done, i + 1)
                for t in range(4):
                    mm = nc.tensor.transpose(pn[:, t], oT[:, t * P:t * P + P], ident[:])
                mm.then_inc(o_turned, 1)

            first_scores(0, 0, 0)
            groups(pe, lambda n, e, m: None, group)

        @block.vector
        def _(dve):
            credit(dve, [(mx_done, UN), (c_dve, 12), (rec_done, 1), (norm_done, 1), (add_done, 1)])

            def maximum(i, u):
                dve.wait_ge(s_done, i * UN + UN + u + 1)
                nc.vector.tensor_reduce(nmx[:, u % 4:u % 4 + 1], pscore[:, u % 4], AX_X, ALU.max, negate=True).then_inc(mx_done, 1)

            def copy(i, u):
                h, qb = divmod(u, 4)
                dve.wait_ge(t_done, i * UN + UN + u + 1)
                if qb == 0:
                    dve.wait_ge(pv_done, i * 4 + 8 + h - 1)
                nc.vector.tensor_copy(alT[:, h % 2, 0:qb + 1, qb * P:qb * P + P], pt[:, u % 2, 0:qb + 1]).then_inc(c_dve, 1)

            def start(n, e, m):
                dve.wait_ge(x_loaded[e], m * 16 + 16)
                dve.sem_inc(passed_d, 1)

            def group(i, g, e, r):
                for u in range(UN):
                    if u + 3 < UN:
                        maximum(i, u + 3)
                    if u % 4 < 3:
                        copy(i, u)
                for u in range(3):
                    maximum(i + 1, u)
                dve.wait_ge(ex_done, i * UN + UN + UN)
                nc.vector.reciprocal(rec[:], sums[:]).then_inc(rec_done, 1)
                dve.wait_ge(rec_done, i + 2)
                dve.wait_ge(o_turned, i + 2)
                nc.vector.tensor_tensor(on[:], pn[:].rearrange("p t (h d) -> p t h d", h=HG)[:, :, :, 0:HD],
                                        rec[:].unsqueeze(3).to_broadcast([P, 4, HG, HD]), ALU.mult).then_inc(norm_done, 1)
                dve.wait_ge(norm_done, i + 2)
                cols = xt[:, e, :, bass.ds(g * 64, 64)]
                nc.vector.tensor_tensor(cols, cols, on[:].rearrange("p t h d -> p t (h d)"), ALU.add).then_inc(add_done, 1)

            for u in range(3):
                maximum(0, u)
            groups(dve, start, group)

        @block.scalar
        def _(act):
            credit(act, [(ex_done, UN), (c_act, 4), (o_put, 1)])

            def copy(i, u):
                h = u // 4
                act.wait_ge(t_done, i * UN + UN + u + 1)
                act.wait_ge(pv_done, i * 4 + 8 + h - 1)
                nc.scalar.copy(alT[:, h % 2, :, 3 * P:], pt[:, u % 2]).then_inc(c_act, 1)

            def group(i, g, e, r):
                act.wait_ge(rec_done, i + 1)
                for u in range(UN):
                    act.wait_ge(mx_done, i * UN + UN + u + 1)
                    act.wait_ge(t_done, i * UN + UN + u - 3)
                    h, qb = divmod(u, 4)
                    nc.scalar.activation(al[:, u % 4], pscore[:, u % 4], ACT.Exp, bias=nmx[:, u % 4:u % 4 + 1],
                                         accum_out=sums[:, qb, h:h + 1]).then_inc(ex_done, 1)
                    if u % 4 == 1 and u > 4:
                        copy(i, u - 2)
                copy(i, UN - 1)
                act.wait_ge(pv_done, i * 4 + 12)
                act.wait_ge(o_turned, i + 1)
                nc.scalar.copy(oT[:], po[:]).then_inc(o_put, 1)

            nc.scalar.preload_act_table_set("exp_and_others")
            groups(act, lambda n, e, m: None, group)


def hybrid_block(nc, x, W_in, W_k, W_v, W_q, W_beta, b_beta, W_out, Wq, Wk, Wv, token, l_gamma, l_w1, l_b1, l_w2, l_b2,
                 h_gamma, h_w1, h_b1, h_w2, h_b2, out):
    T = x.shape[1]
    dram = lambda name, shape, dtype=F32: nc.dram_tensor(name, shape, dtype, kind="Internal").ap()
    kT = dram("kT_dram", (P, 64, T))
    qT = dram("qT_dram", (P, 64, T + 1))
    vbR = dram("vb_dram", (T, 12, 2, 2048), BF16)
    cell = dram("cell_dram", (T + 2 * U, 4, 4, 512))
    rows = dram("xr_dram", (NB * T, 256))
    scores = dram("s_dram", (NB, T))
    lidx = dram("idx_dram", (P, 2 * NB), I32)
    lgate = dram("gate_dram", (P, 2 * NB))
    x2 = dram("x2_dram", (NB * T, 256))
    x3 = dram("x3_dram", (NB, T, 256))
    qk_parts = dram("qk_dram", (NB, 2, HEADS, 3 * HD, T), BF16)
    v_rows = dram("v_dram", (NB * T, HEADS * 32))
    flat = lambda a: a.rearrange("b t d -> (b t) d")

    project_phase(nc, x, W_in, W_k, W_v, W_q, W_beta, b_beta, kT, qT, vbR, T)
    scan_phase(nc, kT, qT, vbR, cell, T)
    light_phase(nc, "la", x, cell, W_out, l_gamma, l_w1, l_b1, l_w2, l_b2, token, x2, rows, scores)
    router_phase(nc, "ra", scores, lidx, lgate)
    heavy_phase(nc, "ha", rows, x2, lidx, lgate, h_gamma, h_w1, h_b1, h_w2, h_b2)
    qkv_phase(nc, "pr", x2, Wq, Wk, Wv, qk_parts, v_rows)
    attention_phase(nc, "at", x2, qk_parts, v_rows, flat(x3))
    light_phase(nc, "lb", x3, None, None, l_gamma, l_w1, l_b1, l_w2, l_b2, token, flat(out), rows, scores)
    router_phase(nc, "rb", scores, lidx, lgate)
    heavy_phase(nc, "hb", rows, flat(out), lidx, lgate, h_gamma, h_w1, h_b1, h_w2, h_b2)


_INS = ['L0_attn_a_x', 'L0_attn_a_W_in', 'L0_attn_a_W_k', 'L0_attn_a_W_v', 'L0_attn_a_W_q', 'L0_attn_a_W_beta',
        'L0_attn_a_b_beta', 'L0_attn_a_W_out', 'L0_attn_b_Wq', 'L0_attn_b_Wk', 'L0_attn_b_Wv', 'L0_ffn_routing_token',
        'L0_ffn_light_gamma', 'L0_ffn_light_w1', 'L0_ffn_light_b1', 'L0_ffn_light_w2', 'L0_ffn_light_b2',
        'L0_ffn_heavy_gamma', 'L0_ffn_heavy_w1', 'L0_ffn_heavy_b1', 'L0_ffn_heavy_w2', 'L0_ffn_heavy_b2']
_OUTS = [((32, 512, 256), 'float32')]


def kernel(**inputs):
    import numpy as _np
    import concourse.bacc as _bacc
    from concourse import mybir as _mybir
    from concourse.bass_utils import run_bass_kernel_spmd as _run

    nc = _bacc.Bacc("TRN2", target_bir_lowering=False, num_devices=1)
    arrays, args = {}, []
    for name in _INS:
        a = _np.ascontiguousarray(inputs[name])
        arrays[f"in_{name}_dram"] = a
        args.append(nc.dram_tensor(f"in_{name}_dram", a.shape, _mybir.dt.from_np(a.dtype), kind="ExternalInput").ap())
    for i, (shape, dtype) in enumerate(_OUTS):
        dt = _mybir.dt.from_np(_np.dtype(dtype))
        args.append(nc.dram_tensor(f"out_{i}_dram", shape, dt, kind="ExternalOutput").ap())
    hybrid_block(nc, *args)
    r = _run(nc, [arrays], core_ids=[0])
    return r.results[0]["out_0_dram"]
```
